# Optimizing a Trainium2 kernel written in Bass

```python
import numpy as np
import jax
import jax.numpy as jnp

def _softmax(x, axis=-1):
    return jax.nn.softmax(x, axis=axis)

def _gelu(x):
    return jax.nn.gelu(x, approximate=True)

def _silu(x):
    return jax.nn.silu(x)

def _sigmoid(x):
    return jax.nn.sigmoid(x)

def _layernorm(x, axis=-1, eps=1e-05):
    m = jnp.mean(x, axis=axis, keepdims=True)
    v = jnp.var(x, axis=axis, keepdims=True)
    return (x - m) / jnp.sqrt(v + eps)

def _scatter_add(tgt, idx, src, axis=0):
    return tgt.at[idx].add(src)

def _segment_sum(src, seg, n):
    return jax.ops.segment_sum(src, seg, n)
kernel_name = 'mk_adj_preln_d4_adj_r2_82f669'

def setup_inputs(seed: int=0):
    np.random.seed(seed)
    _w = jnp.asarray

    def _rec_inputs():
        import jax
        import jax.numpy as jnp
        _gk = jax.random.key(seed)
        x = -0.0005146 + 1 * jax.random.normal(jax.random.fold_in(_gk, 1), (8, 1024, 128), jnp.float32)
        _a = jax.random.bernoulli(jax.random.fold_in(_gk, 2), 0.0078125, (8, 1024, 1024))
        _a = jnp.logical_or(_a, jnp.swapaxes(_a, -1, -2))
        _a = jnp.logical_or(_a, jnp.eye(1024, dtype=bool))
        adj = _a.astype(jnp.int32)
        return (x, adj)
    x, adj = _rec_inputs()

    def _L0_gnn_setup():
        import jax, jax.numpy as jnp
        import numpy as np
        B, N, C, OUT, S = (4, 1024, 128, 128, 25)
        DENSITY = 0.008
        key = jax.random.key(seed)
        kA, kX, kW = jax.random.split(key, 3)
        A = jax.random.bernoulli(kA, DENSITY, (B, N, N)).astype(jnp.int32)
        X = jax.random.normal(kX, (B, N, C), dtype=jnp.float32)
        W = jax.random.normal(kW, (2 * C, OUT), dtype=jnp.float32) * np.float32(1.0 / np.sqrt(2 * C))
        b = jnp.zeros((OUT,), dtype=jnp.float32)
        return {'A': A, 'X': X, 'W': W, 'b': b}
    _L0_gnn_all = _L0_gnn_setup()
    _L0_gnn_in = {k: v for k, v in _L0_gnn_all.items() if k in ('W', 'b')}
    del _L0_gnn_all

    def _L1_gnn_setup():
        import jax, jax.numpy as jnp
        import numpy as np
        NEG_BIG = -9000000000000000.0
        key = jax.random.key(seed)
        k1, k2, k3, k4 = jax.random.split(key, 4)
        B, N, FIN, FOUT = (8, 1024, 128, 128)
        inp = jax.random.normal(k1, (B, N, FIN), dtype=jnp.float32)
        adj = jax.random.randint(k2, (B, N, N), 0, 2, dtype=jnp.int32)
        W = jax.random.normal(k3, (FIN, FOUT), dtype=jnp.float32) * (1.414 / np.sqrt(FIN))
        a = jax.random.normal(k4, (2 * FOUT, 1), dtype=jnp.float32) * 0.1
        return {'input': inp, 'adj': adj, 'W': W, 'a': a}
    _L1_gnn_all = _L1_gnn_setup()
    _L1_gnn_in = {k: v for k, v in _L1_gnn_all.items() if k in ('W', 'a')}
    del _L1_gnn_all

    def _L2_gnn_setup():
        import jax, jax.numpy as jnp
        import numpy as np
        B, N, C_IN, H, C_OUT = (8, 512, 128, 4, 128)
        C = C_OUT // H
        ALPHA = 0.2
        NEG_INF = -9000000000000000.0
        key = jax.random.key(seed)
        k1, k2, k3, k4, k5 = jax.random.split(key, 5)
        node_feats = jax.random.normal(k1, (B, N, C_IN), dtype=jnp.float32)
        adj_matrix = jax.random.randint(k2, (B, N, N), 0, 2, dtype=jnp.int32)
        eye = jnp.eye(N, dtype=jnp.int32)[None]
        adj_matrix = jnp.maximum(adj_matrix, eye)

        def xavier(k, shape, fan_in, fan_out, gain=1.414):
            lim = gain * np.sqrt(6.0 / (fan_in + fan_out))
            return jax.random.uniform(k, shape, jnp.float32, -lim, lim)
        W = xavier(k3, (C_OUT, C_IN), C_IN, C_OUT)
        b = jnp.zeros((C_OUT,), dtype=jnp.float32)
        a = xavier(k4, (H, 2 * C), 2 * C, H)
        return {'node_feats': node_feats, 'adj_matrix': adj_matrix, 'W': W, 'b': b, 'a': a}
    _L2_gnn_all = _L2_gnn_setup()
    _L2_gnn_in = {k: v for k, v in _L2_gnn_all.items() if k in ('W', 'b', 'a')}
    del _L2_gnn_all

    def _L3_gnn_setup():
        import jax, jax.numpy as jnp
        import numpy as np
        NEG_BIG = -9000000000000000.0
        ALPHA = 0.2
        key = jax.random.key(seed)
        k1, k2, k3, k4 = jax.random.split(key, 4)
        B, N, Fin, Fout = (8, 1024, 128, 128)
        h = jax.random.normal(k1, (B, N, Fin), dtype=jnp.float32)
        adj = jax.random.randint(k2, (B, N, N), 0, 2, dtype=jnp.int32)
        limW = 1.414 * np.sqrt(6.0 / (Fin + Fout))
        W = jax.random.uniform(k3, (Fin, Fout), jnp.float32, -limW, limW)
        lima = 1.414 * np.sqrt(6.0 / (2 * Fout + 1))
        a = jax.random.uniform(k4, (2 * Fout, 1), jnp.float32, -lima, lima)
        return {'h': h, 'adj': adj, 'W': W, 'a': a}
    _L3_gnn_all = _L3_gnn_setup()
    _L3_gnn_in = {k: v for k, v in _L3_gnn_all.items() if k in ('W', 'a')}
    del _L3_gnn_all
    return {'x': x, 'adj': adj, 'L0_gnn_W': _L0_gnn_in['W'], 'L0_gnn_b': _L0_gnn_in['b'], 'L1_gnn_W': _L1_gnn_in['W'], 'L1_gnn_a': _L1_gnn_in['a'], 'L2_gnn_W': _L2_gnn_in['W'], 'L2_gnn_b': _L2_gnn_in['b'], 'L2_gnn_a': _L2_gnn_in['a'], 'L3_gnn_W': _L3_gnn_in['W'], 'L3_gnn_a': _L3_gnn_in['a']}

def reference(x, adj, L0_gnn_W, L0_gnn_b, L1_gnn_W, L1_gnn_a, L2_gnn_W, L2_gnn_b, L2_gnn_a, L3_gnn_W, L3_gnn_a):
    import jax
    import jax.numpy as jnp

    def _L0_gnn_ref(A, X, W, b):
        import jax, jax.numpy as jnp
        import numpy as np
        B, N, C, OUT, S = (4, 1024, 128, 128, 25)
        DENSITY = 0.008
        mask = A != 0
        neg_inf = jnp.float32(-jnp.inf)
        pri = -jnp.arange(N, dtype=jnp.float32)
        scores = jnp.where(mask, pri, neg_inf)
        vals, idx = jax.lax.top_k(scores, S)
        valid = vals > neg_inf
        feats = jax.vmap(lambda x, i: x[i])(X, idx)
        feats = jnp.where(valid[..., None], feats, neg_inf)
        agg = feats.max(axis=2)
        degree = mask.sum(axis=-1)
        agg = jnp.where((degree <= S)[..., None], jnp.maximum(agg, 0.0), agg)
        h = jnp.concatenate([X, agg], axis=-1)
        out = jax.nn.relu(jnp.einsum('bnf,fo->bno', h, W) + b)
        return out

    def _L1_gnn_ref(input, adj, W, a):
        import jax, jax.numpy as jnp
        import numpy as np
        NEG_BIG = -9000000000000000.0
        alpha = 0.2
        h = jnp.matmul(input, W)
        F = h.shape[-1]
        a1, a2 = (a[:F, 0], a[F:, 0])
        s1 = jnp.einsum('bnf,f->bn', h, a1)
        s2 = jnp.einsum('bnf,f->bn', h, a2)
        e = s1[:, :, None] + s2[:, None, :]
        e = jax.nn.leaky_relu(e, negative_slope=alpha)
        e = jnp.where(adj > 0, e, NEG_BIG)
        attention = jax.nn.softmax(e, axis=2)
        h_prime = jnp.matmul(attention, h)
        return jax.nn.elu(h_prime)

    def _L2_gnn_ref(node_feats, adj_matrix, W, b, a):
        import jax, jax.numpy as jnp
        import numpy as np
        B, N, C_IN, H, C_OUT = (8, 512, 128, 4, 128)
        C = C_OUT // H
        ALPHA = 0.2
        NEG_INF = -9000000000000000.0
        Bb, Nn, _ = node_feats.shape
        Hh, twoC = a.shape
        Cc = twoC // 2
        h = (node_feats @ W.T + b).reshape(Bb, Nn, Hh, Cc)
        a_src, a_dst = (a[:, :Cc], a[:, Cc:])
        l_src = jnp.einsum('bihc,hc->bih', h, a_src)
        l_dst = jnp.einsum('bjhc,hc->bjh', h, a_dst)
        logits = jax.nn.leaky_relu(l_src[:, :, None, :] + l_dst[:, None, :, :], ALPHA)
        logits = jnp.where(adj_matrix[..., None] == 1, logits, NEG_INF)
        probs = jax.nn.softmax(logits, axis=2)
        out = jnp.einsum('bijh,bjhc->bihc', probs, h)
        return out.reshape(Bb, Nn, Hh * Cc)

    def _L3_gnn_ref(h, adj, W, a):
        import jax, jax.numpy as jnp
        import numpy as np
        NEG_BIG = -9000000000000000.0
        ALPHA = 0.2
        Fout = W.shape[1]
        wh = jnp.einsum('bni,io->bno', h, W)
        a1 = a[:Fout, 0]
        a2 = a[Fout:, 0]
        s1 = wh @ a1
        s2 = wh @ a2
        e = jax.nn.leaky_relu(s1[:, :, None] + s2[:, None, :], negative_slope=ALPHA)
        e = jnp.where(adj > 0, e, NEG_BIG)
        attention = jax.nn.softmax(e, axis=2)
        h_prime = jnp.einsum('bmn,bno->bmo', attention, wh)
        return h_prime
    h = jnp.maximum(_layernorm(x, axis=-1), 0.0)
    x = x + _L0_gnn_ref(adj, h, L0_gnn_W, L0_gnn_b)
    h = jnp.maximum(_layernorm(x, axis=-1), 0.0)
    x = x + _L1_gnn_ref(h, adj, L1_gnn_W, L1_gnn_a)
    h = jnp.maximum(_layernorm(x, axis=-1), 0.0)
    x = x + _L2_gnn_ref(h, adj, L2_gnn_W, L2_gnn_b, L2_gnn_a)
    h = jnp.maximum(_layernorm(x, axis=-1), 0.0)
    x = x + _L3_gnn_ref(h, adj, L3_gnn_W, L3_gnn_a)
    return x

_drawn_inputs = setup_inputs


def setup_inputs(seed=0):
    import zlib

    import numpy as np

    out = dict(_drawn_inputs(seed))
    spreads = {'L0_gnn_b': (0.0, 0.1), 'L2_gnn_b': (0.0, 0.1)}
    factors = {}
    for name, (base, spread) in spreads.items():
        noise = np.random.default_rng([zlib.crc32(name.encode()), seed]).standard_normal(out[name].shape)
        drawn = base * np.exp(spread * noise) if base else spread * noise
        out[name] = jnp.asarray(drawn.astype(out[name].dtype))
    for name, factor in factors.items():
        out[name] = (out[name] * factor).astype(out[name].dtype)
    return out
```

```python
from contextlib import ExitStack

import concourse.bass as bass
from concourse import mybir

P = 128
F32 = mybir.dt.float32
BF16 = mybir.dt.bfloat16
I32 = mybir.dt.int32
U32 = mybir.dt.uint32
ALU = mybir.AluOpType
ACT = mybir.ActivationFunctionType
AX = mybir.AxisListType

S = 25
EPS = 1e-5
SLOPE = 0.2


class Chain:

    def __init__(self, eng, sem):
        self.eng, self.sem, self.n = eng, sem, 0

    def __call__(self, ins):
        self.n += 1
        return ins.then_inc(self.sem, 1)

    def settle(self):
        self.eng.wait_ge(self.sem, self.n)

    def restart(self):
        self.settle()
        self.eng.sem_clear(self.sem)
        self.n = 0


def graph_layers(nc, x, adj, w0, b0, w1, a1, w2, b2, a2, w3, a3, out):
    B, N, C = x.shape
    T = N // P
    HEADS = [0, 1, a2.shape[0], 1]
    G0 = [0, 0, 1, 1 + HEADS[2]]
    NG = sum(HEADS)
    HM = max(HEADS)
    KV = 8 * ((S + 7) // 8)
    ROWS = N + 1
    assert C == P and N % P == 0 and T == 8

    def width(layer):
        return C // HEADS[layer] + 1

    table = nc.dram_tensor("h0_table", (B * ROWS, C), F32).ap()
    table_v = table.rearrange("(b r) c -> b r c", r=ROWS)
    x_v = x.rearrange("b (t p) c -> b p t c", p=P)
    out_v = out.rearrange("b (t p) c -> b p t c", p=P)
    adj_v = adj.rearrange("b (t p) n -> b t p n", p=P)

    with ExitStack() as ctx:
        def sb(name, shape, dt=F32):
            return ctx.enter_context(nc.sbuf_tensor(name, shape, dt))

        def ps(name, shape, dt=F32):
            return ctx.enter_context(nc.psum_tensor(name, shape, dt))

        def sem(name):
            return ctx.enter_context(nc.semaphore(name))

        ident = sb("ident", [P, P])
        ident_bf = sb("ident_bf", [P, P], BF16)
        ones = sb("ones", [P, P])
        descending = sb("descending", [P, N])
        first_row = sb("first_row", [P, 1])
        w0_sb = sb("w0_sb", [P, 2, C])
        b0_row = sb("b0_row", [1, C])
        wr = [None] + [sb(f"wr{l}", [P, C + 3 * HEADS[l]]) for l in (1, 2, 3)]
        wa1 = [None] + [sb(f"wa1_{l}", [P, HEADS[l], P]) for l in (1, 2, 3)]
        b2_row = sb("b2_row", [1, C + 3 * HM])
        b2_col = sb("b2_col", [P, 1])
        adj_in = sb("adj_in", [P, 2, N], I32)
        adj_bf = sb("adj_bf", [P, 2, N], BF16)
        mask_next = sb("mask_next", [P, T, N], BF16)
        mask = sb("mask", [P, T, N], BF16)
        edges = sb("edges", [P, HM, T, N], BF16)
        key = sb("key", [P, N])
        top = sb("top", [P, KV])
        index = sb("index", [P, 4, KV], U32)
        idle = sb("idle", [1, 2])
        gathered = sb("gathered", [P, 2, S * C])
        agg = sb("agg", [P, T, C])
        x_next = sb("x_next", [P, T, C])
        xc = sb("xc", [P, T, C])
        h = sb("h", [P, T, C])
        hT = sb("hT", [P, N])
        aggT = sb("aggT", [P, T * (C + HM)])
        stats = sb("stats", [P, T, 6])
        meanvar = sb("meanvar", [P, T, 2])
        var = sb("var", [P, T])
        std = sb("std", [P, T])
        rstd = sb("rstd", [P, T])
        shift = sb("shift", [P, T])
        wh = sb("wh", [P, T, C + 3 * HM])
        top_s2 = sb("top_s2", [P, HM])
        top_row = sb("top_row", [HM, 1])
        top_diag = sb("top_diag", [HM, HM])
        top_all = sb("top_all", [P, HM])
        s2_rel = sb("s2_rel", [P, T * HM])
        t_neg = sb("t_neg", [P, T * HM])
        t_pos = sb("t_pos", [P, T * HM])
        f1 = sb("f1", [P, T * HM])
        f2 = sb("f2", [P, T * HM])
        f2n = sb("f2n", [P, T * HM])
        e1 = sb("e1", [P, T * HM])
        e2 = sb("e2", [P, T * HM])
        cols = sb("cols", [P, T * 2 * (C + HM)])
        part = [sb(f"part{i}", [P, T * 2 * (C + HM)], BF16) for i in range(3)]
        npart = [sb(f"npart{i}", [P, T * (C + HM)], BF16) for i in range(3)]
        second = sb("second", [P, 2, C + HM])
        numer = aggT
        w_turned = (hT[:, C:2 * C], hT[:, 2 * C:3 * C])
        rden = sb("rden", [P, T * HM])

        ps_mask = ps("ps_mask", [P, T, P], BF16)
        ps_x = ps("ps_x", [P, 2, 512])
        ps_s = ps("ps_s", [P, 2, 512])
        ps_acc = ps("ps_acc", [P, 2, 512])
        ps_small = ps("ps_small", [P, 512])
        ps_w = [ps_acc[:, 0, :], ps_acc[:, 1, :]]
        ps_wa = [ps_small, ps_acc[:, 0, :], ps_acc[:, 1, :]]

        weights_in = sem("weights_in")
        consts_ready = sem("consts_ready")
        diag_ready = sem("diag_ready")
        wprep_ps = sem("wprep_ps")
        wprep_sb = sem("wprep_sb")
        weights_ready = sem("weights_ready")
        x_loaded = sem("x_loaded")
        h0_loaded = sem("h0_loaded")
        table_stored = sem("table_stored")
        out_stored = sem("out_stored")
        adj_loaded = [sem("adj_loaded0"), sem("adj_loaded1")]
        gather_done = [sem("gather_done0"), sem("gather_done1")]
        chain_done = sem("chain_done")
        adj_cast = sem("adj_cast")
        mask_ps = sem("mask_ps")
        mask_next_ready = sem("mask_next_ready")
        mask_ready = sem("mask_ready")
        x_current = sem("x_current")
        index_ready = sem("index_ready")
        idle_done = sem("idle_done")
        gather_free = sem("gather_free")
        var_ready = sem("var_ready")
        std_ready = sem("std_ready")
        norm_ready = sem("norm_ready")
        h_ready = sem("h_ready")
        turned_ps = sem("turned_ps")
        turned_sb = sem("turned_sb")
        sage_ps = sem("sage_ps")
        sage_used = sem("sage_used")
        wh_ps = sem("wh_ps")
        wh_sb = sem("wh_sb")
        s1_ps = sem("s1_ps")
        top_ready = sem("top_ready")
        top_turned = sem("top_turned")
        top_diag_ready = sem("top_diag_ready")
        top_spread = sem("top_spread")
        exp_in_ready = sem("exp_in_ready")
        exp_ready = sem("exp_ready")
        cols_ready = sem("cols_ready")
        hi_ready = sem("hi_ready")
        rest_ready = sem("rest_ready")
        mid_ready = sem("mid_ready")
        lo_ready = sem("lo_ready")
        nparts_ready = sem("nparts_ready")
        edges_ready = sem("edges_ready")
        acc_ready = sem("acc_ready")
        second_ready = sem("second_ready")
        acc_used = sem("acc_used")
        y_ready = sem("y_ready")
        elu_ready = sem("elu_ready")
        x_done = sem("x_done")

        block = ctx.enter_context(nc.Block())
        LOADS = 12 + 4 * HM

        @block.sync
        def _(sp):
            def load(dst, src):
                sp.dma_start(dst, src, allow_slow_non_contiguous=True).then_inc(weights_in, 16)

            def load_adj(b, t):
                if not (isinstance(b, int) and b == 0 and t < 2):
                    sp.wait_ge(adj_cast, b * T + t - 1)
                    sp.wait_ge(index_ready, b * T + t - 1)
                sp.dma_start(adj_in[:, t % 2, :], adj_v[b, t]).then_inc(adj_loaded[t % 2], 16)

            def norm_for_table(k):
                sp.wait_ge(h_ready, k)
                sp.dma_start(x_next[:, :, :], x_v[k]).then_inc(x_loaded, 16)
                sp.wait_ge(h_ready, k + 1)
                sp.dma_start(table_v[k, 0:N, :].rearrange("(t p) c -> p t c", p=P), h[:, :, :])\
                  .then_inc(table_stored, 16)

            def turn(b, more):
                if more:
                    for t in range(T):
                        load_adj(b + 1, t)
                        if t == 2:
                            sp.wait_ge(x_current, b + 1)
                            sp.dma_start(x_next[:, :, :], x_v[b + 1]).then_inc(x_loaded, 16)
                    sp.wait_ge(turned_ps, 10 * (b + 1))
                    sp.dma_start(h[:, :, :], table_v[b + 1, 0:N, :].rearrange("(t p) c -> p t c", p=P))\
                      .then_inc(h0_loaded, 16)
                sp.wait_ge(x_done, b + 1)
                sp.dma_start(out_v[b], xc[:, :, :]).then_inc(out_stored, 16)

            sp.dma_start(x_next[:, :, :], x_v[0]).then_inc(x_loaded, 16)
            load_adj(0, 0)
            load_adj(0, 1)
            load(w0_sb[:, :, :], w0.rearrange("(s k) o -> k s o", k=P))
            load(b0_row[:, :], b0.rearrange("(a n) -> a n", a=1))
            load(b2_row[:, 0:C], b2.rearrange("(a n) -> a n", a=1))
            load(b2_col[:, :], b2.rearrange("(n a) -> n a", a=1))
            load(wr[1][:, 0:C], w1)
            load(wr[3][:, 0:C], w3)
            load(hT[:, 0:C], w2)
            for l, a in ((1, a1), (3, a3)):
                for s in range(2):
                    load(aggT[:, 2 * l + s:2 * l + s + 1], a[s * C:(s + 1) * C, :])
            D = C // HM
            sp.wait_ge(consts_ready, 4)
            for s in range(2):
                for g in range(HM):
                    load(aggT[g * D:(g + 1) * D, 16 + s * HM + g:17 + s * HM + g],
                         a2[g, s * D:(s + 1) * D].rearrange("(d a) -> d a", a=1))
            sp.dma_start(table_v[:, N, :], agg[0:B, 0, :]).then_inc(table_stored, 16)
            sp.wait_ge(table_stored, 16)
            sp.wait_ge(h_ready, 1)
            sp.dma_start(table_v[0, 0:N, :].rearrange("(t p) c -> p t c", p=P), h[:, :, :])\
              .then_inc(table_stored, 16)
            load_adj(0, 2)
            load_adj(0, 3)
            load_adj(0, 4)
            load_adj(0, 5)
            with sp.Fori(1, B) as k:
                norm_for_table(k)
            load_adj(0, 6)
            load_adj(0, 7)
            sp.wait_ge(h_ready, B)
            sp.dma_start(x_next[:, :, :], x_v[0]).then_inc(x_loaded, 16)
            sp.wait_ge(table_stored, 16 * (B + 1))
            sp.dma_start(h[:, :, :], table_v[0, 0:N, :].rearrange("(t p) c -> p t c", p=P))\
              .then_inc(h0_loaded, 16)
            with sp.Fori(0, B - 1) as b:
                turn(b, True)
            turn(B - 1, False)
            sp.wait_ge(out_stored, 16 * B)

        @block.gpsimd
        def _(pool):
            nc.gpsimd.iota(descending[:, :], pattern=[[-1, N]], base=N, channel_multiplier=0,
                           allow_small_or_imprecise_dtypes=True).then_inc(diag_ready, 1)
            nc.gpsimd.memset(idle[:, :], 0.0).then_inc(diag_ready, 1)
            pool.wait_ge(diag_ready, 2)
            pool.wait_ge(consts_ready, 2)
            for m in (ident, ident_bf):
                nc.gpsimd.affine_select(out=m[:, :], in_=m[:, :], compare_op=ALU.not_equal, fill=1.0, base=0,
                                        pattern=[[-1, P]], channel_multiplier=1).then_inc(diag_ready, 1)
            pool.wait_ge(table_stored, 16 * (B + 1))
            with pool.Fori(0, B) as b:
                for t in range(T):
                    pool.wait_ge(index_ready, b * T + t + 1)
                    nc.gpsimd.tensor_tensor(idle[:, 1:2], idle[:, 0:1], idle[:, 0:1], ALU.add)\
                      .then_inc(idle_done, 1)
                    pool.wait_ge(gather_free, 1)
                    pool.wait_ge(gather_free, b * T + t + 1)
                    pool.wait_ge(idle_done, b * T + t + 1)
                    for k in range(S):
                        nc.gpsimd.indirect_dma_start(
                            out=gathered[:, t % 2, k * C:(k + 1) * C], out_offset=None, in_=table,
                            in_offset=bass.IndirectOffsetOnAxis(ap=index[:, t % 4, k:k + 1], axis=0),
                        ).then_inc(gather_done[t % 2], 16)

        @block.vector
        def _(dve):
            step = Chain(dve, chain_done)

            def norm(src, L):
                for t in range(T):
                    step(nc.vector.bn_stats(out=stats[:, t, :], in_=src[:, t, :]))
                step.settle()
                for t in range(T):
                    step(nc.vector.bn_aggr(out=meanvar[:, t, :], in_=stats[:, t, :]))
                step.settle()
                nc.vector.tensor_scalar(var[:, :], meanvar[:, :, 1], EPS, None, ALU.add).then_inc(var_ready, 1)
                dve.wait_ge(std_ready, L + 1)
                step(nc.vector.reciprocal(rstd[:, :], std[:, :]))
                step.settle()
                nc.vector.scalar_tensor_tensor(out=shift[:, :], in0=meanvar[:, :, 0], scalar=-1.0, in1=rstd[:, :],
                                               op0=ALU.mult, op1=ALU.mult).then_inc(norm_ready, 1)

            def list_neighbours(b, t):
                dve.wait_ge(adj_loaded[t % 2], b * (16 * T // 2) + 16 * (t // 2 + 1))
                step(nc.vector.tensor_tensor(key[:, :], adj_in[:, t % 2, :], descending[:, :], ALU.mult))
                step.settle()
                for r in range(KV // 8):
                    eight = top[:, 8 * r:8 * r + 8]
                    step(nc.vector.max(out=eight, in_=key[:, :]))
                    step.settle()
                    if r < KV // 8 - 1:
                        step(nc.vector.match_replace(out=key[:, :], in_to_replace=eight, in_values=key[:, :],
                                                     imm_value=0.0))
                        step.settle()
                nc.vector.tensor_scalar(index[:, t % 4, :], top[:, :], -1.0, first_row[:, 0:1], ALU.mult, ALU.add)\
                  .then_inc(index_ready, 1)

            def take_maximum(b, t):
                dve.wait_ge(gather_done[t % 2], b * (16 * S * T // 2) + 16 * S * (t // 2 + 1))
                nc.vector.tensor_reduce(agg[:, t, :], gathered[:, t % 2, :].rearrange("p (k c) -> p c k", k=S),
                                        AX.X, ALU.max).then_inc(gather_free, 1)

            def attention(b, layer, fill):
                H, D1 = HEADS[layer], width(layer)
                D = D1 - 1
                m = b * 3 + (layer - 1)
                HT = T * H
                s1 = wh[:, :, C:C + H]
                s2 = wh[:, :, C + H:C + 2 * H]
                minus_s2 = wh[:, :, C + 2 * H:C + 3 * H]

                def small(tile):
                    return tile[:, 0:HT].rearrange("p (t h) -> p t h", h=H)

                dve.wait_ge(wh_sb, b * 24 + 8 * layer)
                nc.vector.tensor_reduce(top_s2[:, 0:H], s2.rearrange("p t h -> p h t"), AX.X, ALU.max)\
                  .then_inc(top_ready, 1)
                dve.wait_ge(top_turned, m + 1)
                step(nc.vector.tensor_reduce(top_row[0:H, :], ps_small[0:H, 0:P], AX.X, ALU.max))
                step.settle()
                nc.vector.tensor_scalar(top_diag[0:H, 0:H], ident[0:H, 0:H], top_row[0:H, 0:1], None, ALU.mult)\
                  .then_inc(top_diag_ready, 1)
                dve.wait_ge(top_spread, m + 1)
                step(nc.vector.tensor_copy(top_all[:, 0:H], ps_small[:, 0:H]))
                step.settle()
                spread = top_all[:, 0:H].unsqueeze(1).to_broadcast([P, T, H])
                step(nc.vector.tensor_tensor(small(s2_rel), s2, spread, ALU.subtract))
                step(nc.vector.tensor_tensor(small(rden), s1, spread, ALU.add))
                step.settle()
                nc.vector.tensor_scalar(t_neg[:, 0:HT], rden[:, 0:HT], 0.0, None, ALU.min).then_inc(exp_in_ready, 1)
                nc.vector.tensor_scalar(t_pos[:, 0:HT], rden[:, 0:HT], 0.0, None, ALU.max).then_inc(exp_in_ready, 1)

                def mark_edges(g, tiles):
                    dve.wait_ge(s1_ps, b * NG + G0[layer] + g + 1)
                    row = (ps_s, ps_x)[(G0[layer] + g) % 2]
                    for t in tiles:
                        ins = nc.vector.scalar_tensor_tensor(
                            out=edges[:, g, t, :], in0=row[:, :, :].rearrange("p a n -> p (a n)"),
                            scalar=minus_s2[:, t, g:g + 1], in1=mask[:, t, :], op0=ALU.is_gt, op1=ALU.mult)
                    if t == T - 1:
                        ins.then_inc(edges_ready, 1)

                mark_edges(0, range(0, 3))
                dve.wait_ge(exp_ready, m + 1)
                step(nc.vector.tensor_scalar(f2n[:, 0:HT], f2[:, 0:HT], -1.0, None, ALU.mult))
                step.settle()
                cv = cols[:, 0:HT * 2 * D1].rearrange("p (t h s d) -> p t h s d", h=H, s=2, d=D1)
                whv = wh[:, :, 0:C].rearrange("p t (h d) -> p t h d", d=D)
                for s, f in enumerate((f1, f2n)):
                    step(nc.vector.tensor_tensor(cv[:, :, :, s, 0:D], whv,
                                                 small(f).unsqueeze(3).to_broadcast([P, T, H, D]), ALU.mult))
                    ins = nc.vector.tensor_copy(cv[:, :, :, s, D], small(f))
                    if s:
                        ins.then_inc(cols_ready, 1)
                    else:
                        step(ins)
                step.settle()
                W = HT * 2 * D1
                mark_edges(0, range(3, 6))
                dve.wait_ge(hi_ready, m + 1)
                nc.vector.tensor_tensor(cols[:, 0:W], cols[:, 0:W], part[0][:, 0:W], ALU.subtract)\
                  .then_inc(rest_ready, 1)
                mark_edges(0, range(6, 8))
                dve.wait_ge(mid_ready, m + 1)
                dve.wait_ge(rest_ready, m + 1)
                nc.vector.tensor_tensor(part[2][:, 0:W], cols[:, 0:W], part[1][:, 0:W], ALU.subtract)\
                  .then_inc(lo_ready, 1)
                for g in range(1, H):
                    mark_edges(g, range(T))

                for t in range(T):
                    if t in fill:
                        fill[t]()
                    n = b * 24 + 8 * (layer - 1) + t
                    dve.wait_ge(second_ready, n + 1)
                    acc = ps_acc[:, t % 2, 0:2 * H * D1].rearrange("p (h s d) -> p h s d", h=H, s=2)
                    for g in range(H):
                        ins = nc.vector.scalar_tensor_tensor(
                            out=numer[:, (t * H + g) * D1:(t * H + g + 1) * D1], in0=acc[:, g, 0, :],
                            scalar=e1[:, t * H + g:t * H + g + 1], in1=second[:, t % 2, g * D1:(g + 1) * D1],
                            op0=ALU.mult, op1=ALU.add)
                    ins.then_inc(acc_used, 1)
                dve.wait_ge(acc_used, b * 24 + 8 * layer)
                nv = numer[:, 0:HT * D1].rearrange("p (t h d) -> p t h d", h=H, d=D1)
                step(nc.vector.reciprocal(small(rden), nv[:, :, :, D]))
                step.settle()
                y = h[:, :, :].rearrange("p t (h d) -> p t h d", d=D)
                hf = h[:, :, :].rearrange("p t c -> p (t c)")
                xf = xc[:, :, :].rearrange("p t c -> p (t c)")
                step(nc.vector.tensor_tensor(nv[:, :, :, 0:D], nv[:, :, :, 0:D],
                                             small(rden).unsqueeze(3).to_broadcast([P, T, H, D]), ALU.mult))
                step.settle()
                xv = xc[:, :, :].rearrange("p t (h d) -> p t h d", d=D)
                if layer == 1:
                    nc.vector.tensor_scalar(y, nv[:, :, :, 0:D], 0.0, None, ALU.min).then_inc(y_ready, 1)
                    for t in range(T):
                        ins = nc.vector.scalar_tensor_tensor(out=xc[:, t, :], in0=nv[:, t, 0, 0:D], scalar=0.0,
                                                             in1=xc[:, t, :], op0=ALU.max, op1=ALU.add)
                        step(ins)
                    step.settle()
                    dve.wait_ge(elu_ready, b + 1)
                    step(nc.vector.scalar_tensor_tensor(out=xf, in0=hf, scalar=-1.0, in1=xf,
                                                        op0=ALU.add, op1=ALU.add))
                    step.settle()
                elif layer == 2:
                    step(nc.vector.tensor_tensor(xv, xv, nv[:, :, :, 0:D], ALU.add))
                    step.settle()
                else:
                    nc.vector.tensor_tensor(xv, xv, nv[:, :, :, 0:D], ALU.add).then_inc(x_done, 1)

            def bring_forward(b):
                dve.wait_ge(mask_next_ready, b * T + T)
                nc.vector.tensor_copy(mask[:, :, :], mask_next[:, :, :]).then_inc(mask_ready, 1)
                dve.wait_ge(x_loaded, b * 16 + 16 * (B + 1))
                if not isinstance(b, int):
                    dve.wait_ge(out_stored, b * 16)
                nc.vector.tensor_copy(xc[:, :, :], x_next[:, :, :]).then_inc(x_current, 1)

            def turn(b, more):
                if more:
                    step(nc.vector.tensor_scalar(first_row[:, :], first_row[:, :], float(ROWS), None, ALU.add))
                    step.settle()
                    list_neighbours(b + 1, 0)
                    list_neighbours(b + 1, 1)
                take_maximum(b, 6)
                if more:
                    list_neighbours(b + 1, 2)
                take_maximum(b, 7)
                if more:
                    list_neighbours(b + 1, 3)
                for t in range(T):
                    dve.wait_ge(sage_ps, b * T + t + 1)
                    if t == 0:
                        dve.wait_ge(x_current, b + 1)
                    nc.vector.scalar_tensor_tensor(out=xc[:, t, :], in0=ps_w[t % 2][:, 0:C], scalar=0.0,
                                                   in1=xc[:, t, :], op0=ALU.max, op1=ALU.add).then_inc(sage_used, 1)
                dve.wait_ge(sage_used, b * T + T)
                norm(xc, b * 3 + B)
                attention(b, 1, {0: lambda: take_maximum(b + 1, 0), 3: lambda: list_neighbours(b + 1, 4),
                                 6: lambda: take_maximum(b + 1, 1)} if more else {})
                norm(xc, b * 3 + B + 1)
                attention(b, 2, {0: lambda: (list_neighbours(b + 1, 5), take_maximum(b + 1, 2)),
                                 4: lambda: list_neighbours(b + 1, 6)} if more else {})
                norm(xc, b * 3 + B + 2)
                attention(b, 3, {0: lambda: take_maximum(b + 1, 3), 3: lambda: list_neighbours(b + 1, 7),
                                 6: lambda: (take_maximum(b + 1, 4), take_maximum(b + 1, 5))} if more else {})
                if more:
                    bring_forward(b + 1)

            nc.vector.memset(ident[:, :], 0.0).then_inc(consts_ready, 1)
            nc.vector.memset(ident_bf[:, :], 0.0).then_inc(consts_ready, 1)
            nc.vector.memset(agg[:, 0, :], 0.0).then_inc(consts_ready, 1)
            nc.vector.memset(aggT[:, 16:64], 0.0).then_inc(consts_ready, 1)
            nc.vector.memset(first_row[:, :], float(N)).then_inc(gather_free, 2)
            step(nc.vector.memset(ones[:, :], 1.0))
            step.settle()
            dve.wait_ge(x_loaded, 16)
            norm(x_next, 0)
            dve.wait_ge(diag_ready, 1)
            dve.wait_ge(gather_free, 2)
            for t in range(4):
                list_neighbours(0, t)

            step.restart()
            with dve.Fori(1, B) as k:
                dve.wait_ge(x_loaded, k * 16 + 16)
                norm(x_next, k)
                step.restart()
            for n, l in enumerate((1, 3, 2)):
                H = HEADS[l]
                if l == 2:
                    dve.wait_ge(wprep_ps, 5)
                    step(nc.vector.tensor_copy(wr[2][:, 0:C], ps_x[:, 0, 0:C]))
                    step(nc.vector.tensor_copy(b2_row[:, C:C + 2 * H], ps_wa[2][0:1, 64:64 + 2 * H]))
                    step.settle()
                    step(nc.vector.scalar_tensor_tensor(
                        out=b2_row[:, C + 2 * H:C + 3 * H], in0=b2_row[:, C:C + H], scalar=-1.0,
                        in1=b2_row[:, C + H:C + 2 * H], op0=ALU.mult, op1=ALU.subtract))
                else:
                    dve.wait_ge(wprep_ps, 2 * n + 1)
                    nc.vector.tensor_copy(w_turned[n], ps_x[:, n, 0:C]).then_inc(wprep_sb, 1)
                    dve.wait_ge(wprep_ps, 2 * n + 2)
                step(nc.vector.tensor_copy(wr[l][:, C:C + 2 * H], ps_wa[n][:, 0:2 * H]))
                step(nc.vector.tensor_scalar(wr[l][:, C + 2 * H:C + 3 * H], ps_wa[n][:, H:2 * H],
                                             -1.0, None, ALU.mult))
                step.settle()
                for g in range(H):
                    nc.vector.tensor_scalar(wa1[l][:, g, :], ones[:, :], wr[l][:, C + g:C + g + 1], None,
                                            ALU.mult).then_inc(weights_ready, 1)

            take_maximum(0, 0)
            take_maximum(0, 1)
            for t in range(4, T):
                list_neighbours(0, t)
                take_maximum(0, t - 2)
            bring_forward(0)
            step.restart()
            with dve.Fori(0, B - 1) as b:
                turn(b, True)
                step.restart()
            turn(B - 1, False)

        @block.scalar
        def _(act):
            def norm(src, L, before=None):
                act.wait_ge(var_ready, L + 1)
                nc.scalar.activation(std[:, :], var[:, :], ACT.Sqrt).then_inc(std_ready, 1)
                act.wait_ge(norm_ready, L + 1)
                if before is not None:
                    act.wait_ge(table_stored, before)
                for t in range(T):
                    ins = nc.scalar.activation(h[:, t, :], src[:, t, :], ACT.Relu, bias=shift[:, t:t + 1],
                                               scale=rstd[:, t:t + 1])
                ins.then_inc(h_ready, 1)

            def cast_mask(b, t):
                n = b * T + t
                act.wait_ge(adj_loaded[t % 2], b * (16 * T // 2) + 16 * (t // 2 + 1))
                if not (isinstance(b, int) and b == 0 and t < 2):
                    act.wait_ge(mask_ps, n - 1)
                nc.scalar.activation(adj_bf[:, t % 2, :], adj_in[:, t % 2, :], ACT.Copy).then_inc(adj_cast, 1)

            def keep_mask(b, t):
                act.wait_ge(mask_ps, b * T + t + 1)
                if t == 0:
                    act.wait_ge(mask_ready, b)
                nc.scalar.activation(mask_next[:, :, t * P:(t + 1) * P], ps_mask[:, :, :], ACT.Copy)\
                  .then_inc(mask_next_ready, 1)

            def keep_turned(b, s, dst):
                for half in range(2):
                    act.wait_ge(turned_ps, b * 10 + 2 * s + half + 1)
                    nc.scalar.activation(dst[:, half * 512:(half + 1) * 512], ps_x[:, half, :], ACT.Copy)\
                      .then_inc(turned_sb, 1)

            def attention(b, layer):
                H, D1 = HEADS[layer], width(layer)
                m = b * 3 + (layer - 1)
                HT, W = T * H, 2 * T * H * D1
                keep_turned(b, layer + 1, hT)
                for t in range(T):
                    act.wait_ge(wh_ps, b * 24 + 8 * (layer - 1) + t + 1)
                    nc.scalar.activation(wh[:, t, 0:C + 3 * H], ps_w[t % 2][:, 0:C + 3 * H], ACT.Copy)\
                      .then_inc(wh_sb, 1)
                act.wait_ge(exp_in_ready, b * 6 + 2 * layer)
                nc.scalar.activation(f1[:, 0:HT], s2_rel[:, 0:HT], ACT.Exp)
                nc.scalar.activation(f2[:, 0:HT], s2_rel[:, 0:HT], ACT.Exp, scale=SLOPE)
                nc.scalar.activation(e1[:, 0:HT], t_neg[:, 0:HT], ACT.Exp, scale=1.0 - SLOPE)
                nc.scalar.activation(e2[:, 0:HT], t_pos[:, 0:HT], ACT.Exp, scale=SLOPE - 1.0)\
                  .then_inc(exp_ready, 1)
                act.wait_ge(cols_ready, m + 1)
                nc.scalar.activation(part[0][:, 0:W], cols[:, 0:W], ACT.Copy).then_inc(hi_ready, 1)
                act.wait_ge(rest_ready, m + 1)
                nc.scalar.activation(part[1][:, 0:W], cols[:, 0:W], ACT.Copy).then_inc(mid_ready, 1)
                act.wait_ge(mid_ready, m + 1)
                act.wait_ge(lo_ready, m + 1)
                for i in range(3):
                    pv = part[i][:, 0:W].rearrange("p (q s d) -> p q s d", s=2, d=D1)
                    ins = nc.scalar.mul(npart[i][:, 0:W // 2].rearrange("p (q d) -> p q d", d=D1),
                                        pv[:, :, 1, :], -1.0)
                ins.then_inc(nparts_ready, 1)

            def second_half(b, layer, t):
                H, D1 = HEADS[layer], width(layer)
                n = b * 24 + 8 * (layer - 1) + t
                act.wait_ge(acc_ready, n + 1)
                if t >= 2:
                    act.wait_ge(acc_used, n - 1)
                acc = ps_acc[:, t % 2, 0:2 * H * D1].rearrange("p (h s d) -> p h s d", h=H, s=2)
                for g in range(H):
                    ins = nc.scalar.activation(second[:, t % 2, g * D1:(g + 1) * D1], acc[:, g, 1, :],
                                               ACT.Copy, scale=e2[:, t * H + g:t * H + g + 1])
                ins.then_inc(second_ready, 1)

            def turn(b, more):
                def new_mask(t):
                    if more:
                        cast_mask(b + 1, t)
                        keep_mask(b + 1, t)

                for t in range(4):
                    new_mask(t)
                keep_turned(b, 0, hT)
                keep_turned(b, 1, aggT)
                for layer in (1, 2, 3):
                    norm(xc, b * 3 + B + layer - 1)
                    attention(b, layer)
                    for t in range(T):
                        if (layer, t) in ((1, 3), (2, 0), (2, 4), (3, 3)):
                            new_mask({(1, 3): 4, (2, 0): 5, (2, 4): 6, (3, 3): 7}[layer, t])
                        second_half(b, layer, t)
                    if layer == 1:
                        act.wait_ge(y_ready, b + 1)
                        nc.scalar.activation(h[:, :, :], h[:, :, :], ACT.Exp).then_inc(elu_ready, 1)

            norm(x_next, 0)
            for t in range(4):
                cast_mask(0, t)
                keep_mask(0, t)
            with act.Fori(1, B) as k:
                norm(x_next, k, k * 16 + 16)
            for t in range(4, T):
                cast_mask(0, t)
                keep_mask(0, t)
            with act.Fori(0, B - 1) as b:
                turn(b, True)
            turn(B - 1, False)

        @block.tensor
        def _(pe):
            def turn_mask(b, t):
                n = b * T + t
                pe.wait_ge(adj_cast, n + 1)
                pe.wait_ge(mask_next_ready, n)
                for j in range(T):
                    ins = nc.tensor.transpose(ps_mask[:, j, :], adj_bf[:, t % 2, j * P:(j + 1) * P], ident_bf[:, :])
                ins.then_inc(mask_ps, 1)

            def turn_features(b, s, src):
                for half in range(2):
                    if s:
                        pe.wait_ge(turned_sb, b * 10 + 2 * s + half - 1)
                    for t in range(4):
                        ins = nc.tensor.transpose(ps_x[:, half, t * P:(t + 1) * P], src[:, 4 * half + t, :],
                                                  ident[:, :])
                    ins.then_inc(turned_ps, 1)

            def sage(b):
                pe.wait_ge(h0_loaded, b * 16 + 16)
                turn_features(b, 0, h)
                pe.wait_ge(gather_free, b * T + T + 2)
                turn_features(b, 1, agg)
                pe.wait_ge(turned_sb, b * 10 + 4)
                for t in range(T):
                    if t >= 2:
                        pe.wait_ge(sage_used, b * T + t - 1)
                    o = ps_w[t % 2][:, 0:C]
                    nc.tensor.matmul(o, hT[:, t * P:(t + 1) * P], w0_sb[:, 0, :], start=True, stop=False)
                    nc.tensor.matmul(o, aggT[:, t * P:(t + 1) * P], w0_sb[:, 1, :], start=False, stop=False)
                    nc.tensor.matmul(o, ones[0:1, :], b0_row[:, :], start=False, stop=True).then_inc(sage_ps, 1)

            def attention(b, layer, fill):
                H, D1 = HEADS[layer], width(layer)
                m = b * 3 + (layer - 1)
                WW = C + 3 * H
                pe.wait_ge(h_ready, m + B + 1)
                turn_features(b, layer + 1, h)
                pe.wait_ge(turned_sb, b * 10 + 2 * layer + 4)
                for t in range(T):
                    n = b * 24 + 8 * (layer - 1) + t
                    if t >= 2:
                        pe.wait_ge(wh_sb, n - 1)
                    o = ps_w[t % 2][:, 0:WW]
                    ins = nc.tensor.matmul(o, hT[:, t * P:(t + 1) * P], wr[layer][:, :], start=True, stop=layer != 2)
                    if layer == 2:
                        ins = nc.tensor.matmul(o, ones[0:1, :], b2_row[:, 0:WW], start=False, stop=True)
                    ins.then_inc(wh_ps, 1)

                def spread_s1(g):
                    k = G0[layer] + g
                    if g >= 2:
                        pe.wait_ge(edges_ready, b * NG + k - 1)
                    row = (ps_s, ps_x)[k % 2]
                    for half in range(2):
                        ins = nc.tensor.matmul(row[:, half, :], wa1[layer][:, g, :],
                                               hT[:, half * 512:(half + 1) * 512], start=True, stop=True)
                    ins.then_inc(s1_ps, 1)

                for g in range(min(H, 2)):
                    spread_s1(g)
                pe.wait_ge(top_ready, m + 1)
                nc.tensor.transpose(ps_small[0:H, 0:P], top_s2[:, 0:H], ident[:, :]).then_inc(top_turned, 1)
                pe.wait_ge(top_diag_ready, m + 1)
                nc.tensor.matmul(ps_small[:, 0:H], ones[0:H, :], top_diag[0:H, 0:H], start=True, stop=True)\
                  .then_inc(top_spread, 1)
                for g in range(2, H):
                    spread_s1(g)
                pe.wait_ge(nparts_ready, m + 1)
                pe.wait_ge(edges_ready, b * NG + G0[layer] + H)
                Q = 2 * H * D1
                for i in range(T):
                    if i in fill:
                        fill[i]()
                    n = b * 24 + 8 * (layer - 1) + i
                    if i >= 2:
                        pe.wait_ge(acc_used, n - 1)
                    acc = ps_acc[:, i % 2, 0:Q]
                    acc_v = acc.rearrange("p (h s d) -> p h s d", h=H, s=2)
                    for j in range(T):
                        for g in range(H):
                            for k in range(3):
                                at = j * Q + g * 2 * D1
                                nc.tensor.matmul(acc[:, g * 2 * D1:(g + 1) * 2 * D1],
                                                 edges[:, g, j, i * P:(i + 1) * P], part[k][:, at:at + 2 * D1],
                                                 start=(j == g == k == 0), stop=False, skip_group_check=True)
                        for k in range(3):
                            ins = nc.tensor.matmul(acc_v[:, :, 1, :], mask[:, j, i * P:(i + 1) * P],
                                                   npart[k][:, j * (Q // 2):(j + 1) * (Q // 2)]
                                                   .rearrange("p (h d) -> p h d", h=H),
                                                   start=False, stop=(j == T - 1 and k == 2), skip_group_check=True)
                    ins.then_inc(acc_ready, 1)

            def turn(b, more):
                if more:
                    for t in range(4):
                        turn_mask(b + 1, t)
                sage(b)
                attention(b, 1, {3: lambda: turn_mask(b + 1, 4)} if more else {})
                attention(b, 2, {0: lambda: turn_mask(b + 1, 5), 4: lambda: turn_mask(b + 1, 6)} if more else {})
                attention(b, 3, {3: lambda: turn_mask(b + 1, 7)} if more else {})

            pe.wait_ge(diag_ready, 4)
            for t in range(4):
                turn_mask(0, t)
            pe.wait_ge(weights_in, 16 * (11 + 2 * HM))
            for n, l in enumerate((1, 3)):
                nc.tensor.transpose(ps_x[:, n, 0:C], wr[l][:, 0:C], ident[:, :]).then_inc(wprep_ps, 1)
                pe.wait_ge(wprep_sb, n + 1)
                nc.tensor.matmul(ps_wa[n][:, 0:2], w_turned[n], aggT[:, 2 * l:2 * l + 2],
                                 start=True, stop=True).then_inc(wprep_ps, 1)
            block_diag = aggT[:, 16:16 + 2 * HM]
            nc.tensor.matmul(ps_wa[2][:, 0:2 * HM], hT[:, 0:C], block_diag, start=True, stop=True)
            nc.tensor.matmul(ps_wa[2][0:1, 64:64 + 2 * HM], b2_col[:, 0:1], block_diag, start=True, stop=True)
            pe.wait_ge(wprep_sb, 1)
            nc.tensor.transpose(ps_x[:, 0, 0:C], hT[:, 0:C], ident[:, :]).then_inc(wprep_ps, 1)
            for t in range(4, T):
                turn_mask(0, t)
            pe.wait_ge(weights_ready, NG)
            with pe.Fori(0, B - 1) as b:
                turn(b, True)
            turn(B - 1, False)


_INS = ['x', 'adj', 'L0_gnn_W', 'L0_gnn_b', 'L1_gnn_W', 'L1_gnn_a', 'L2_gnn_W', 'L2_gnn_b', 'L2_gnn_a', 'L3_gnn_W',
        'L3_gnn_a']
_OUTS = [((8, 1024, 128), 'float32')]


def kernel(**inputs):
    import numpy as _np
    import concourse.bacc as _bacc
    from concourse import mybir as _mybir
    from concourse.bass_utils import run_bass_kernel_spmd as _run

    nc = _bacc.Bacc("TRN2", target_bir_lowering=False, num_devices=1)
    arrays, args = {}, []
    for name in _INS:
        a = _np.ascontiguousarray(inputs[name])
        arrays[f"in_{name}_dram"] = a
        args.append(nc.dram_tensor(f"in_{name}_dram", a.shape, _mybir.dt.from_np(a.dtype), kind="ExternalInput").ap())
    for i, (shape, dtype) in enumerate(_OUTS):
        dt = _mybir.dt.from_np(_np.dtype(dtype))
        args.append(nc.dram_tensor(f"out_{i}_dram", shape, dt, kind="ExternalOutput").ap())
    graph_layers(nc, *args)
    r = _run(nc, [arrays], core_ids=[0])
    got = tuple(r.results[0][f"out_{i}_dram"] for i in range(len(_OUTS)))
    return got[0]
```

```python
from contextlib import ExitStack

import concourse.bass as bass
from concourse import mybir

P = 128
F32 = mybir.dt.float32
BF16 = mybir.dt.bfloat16
I32 = mybir.dt.int32
U32 = mybir.dt.uint32
ALU = mybir.AluOpType
ACT = mybir.ActivationFunctionType
AX = mybir.AxisListType

S = 25
EPS = 1e-5
SLOPE = 0.2
RSQRT_SEED = 0x5F3759DF
STEEP = 2.0 ** 100


class Chain:

    def __init__(self, eng, sem):
        self.eng, self.sem, self.n = eng, sem, 0

    def __call__(self, ins):
        self.n += 1
        return ins.then_inc(self.sem, 1)

    def settle(self):
        self.eng.wait_ge(self.sem, self.n)

    def restart(self):
        self.settle()
        self.eng.sem_clear(self.sem)
        self.n = 0


def graph_layers(nc, x, adj, w0, b0, w1, a1, w2, b2, a2, w3, a3, out):
    B, N, C = x.shape
    T = N // P
    HEADS = [0, 1, a2.shape[0], 1]
    HM = max(HEADS)
    G0 = [0, 0, 1, 1 + HM]
    NG = sum(HEADS)
    GROUPS = [0, 1, 2, 1]
    A0 = [0, 0, T, 3 * T]
    NA = 4 * T
    QUAD = 4
    Q = N // QUAD
    KV = 8 * ((S + 7) // 8)
    ROWS = N + 1
    CH = 2
    TC = T // CH
    assert C == P and N % P == 0 and T == 8 and HM == 4 and B % 2 == 0

    H0_TURNS = (2, 3, 4)
    H0_PRODUCTS = 6

    def width(layer):
        return C // HEADS[layer] + 1

    def second_group(layer, i):
        if layer != 2 or not 0 < i < T - 1:
            return []
        return [(HM // 2 + q // T, q % T) for q in range((i - 1) * 8 // 3, min(i * 8 // 3, 2 * T))]

    def shared(k):
        return k != G0[2]

    def rough_count(k, t):
        return (k - (k > G0[2])) * T + t + 1

    LISTS = {
        (1, -1): [(0, 1)], (1, 0): [(1, 0)], (1, 1): [(1, 1)], (1, 2): [(2, 0)], (1, 4): [(2, 1)],
        (1, 6): [(3, 0)], (2, -1): [(3, 1)], (2, 0): [(4, 0)], (2, 1): [(4, 1)], (2, 8): [(5, 0)], (2, 10): [(5, 1)],
        (2, 12): [(6, 0)], (2, 14): [(6, 1)], (3, 0): [(7, 0)], (3, 1): [(7, 1)],
    }
    MAXIMA = {(1, 3): 0, (1, 7): 1, (2, 2): 2, (2, 9): 3, (3, -1): 4, (3, 2): 5, (3, 5): 6}
    TURNS = {(1, 0): 2, (1, 3): 3, (1, 7): 4, (2, 3): 5, (2, 9): 6, (2, 14): 7}
    CODES = {(1, 0): 1, (1, 2): 2, (1, 6): 3, (2, 0): 4, (2, 8): 5, (2, 12): 6, (3, 0): 7}

    table = nc.dram_tensor("h0_table", (B * ROWS, C), F32).ap()
    table_v = table.rearrange("(b r) c -> b r c", r=ROWS)
    x_v = x.rearrange("b (t p) c -> b p t c", p=P)
    out_v = out.rearrange("b (t p) c -> b p t c", p=P)
    adj_v = adj.rearrange("b (t p) n -> b t p n", p=P)

    with ExitStack() as ctx:
        def sb(name, shape, dt=F32):
            return ctx.enter_context(nc.sbuf_tensor(name, shape, dt))

        def ps(name, shape, dt=F32):
            return ctx.enter_context(nc.psum_tensor(name, shape, dt))

        def sem(name):
            return ctx.enter_context(nc.semaphore(name))

        ident = sb("ident", [P, P])
        ident_bf = sb("ident_bf", [P, P], BF16)
        ones = sb("ones", [P, P])
        quad_bits = sb("quad_bits", [P, P // QUAD], BF16)
        code_base = sb("code_base", [P, Q])
        bit_of = sb("bit_of", [P, QUAD], I32)
        place = sb("place", [P, QUAD])
        first_row = sb("first_row", [P, 1])
        w0_sb = sb("w0_sb", [P, 2, C])
        b0_row = sb("b0_row", [1, C])
        wr = [None] + [sb(f"wr{l}", [P, C + 3 * HEADS[l]]) for l in (1, 2, 3)]
        wa1 = [None] + [sb(f"wa1_{l}", [P, HEADS[l], P]) for l in (1, 2, 3)]
        b2_row = sb("b2_row", [1, C + 3 * HM])
        b2_col = sb("b2_col", [P, 1])
        adj_in = sb("adj_in", [P, 2, N], I32)
        adj_bf = sb("adj_bf", [P, 2, N], BF16)
        mask_next = sb("mask_next", [P, T, N], BF16)
        mask = sb("mask", [P, T, N], BF16)
        edges = sb("edges", [P, HM, T, N], BF16)
        codes = sb("codes", [P, Q])
        top = sb("top", [P, KV])
        top_int = sb("top_int", [P, KV], I32)
        quad_up = sb("quad_up", [P, KV], I32)
        bits = sb("bits", [P, KV, QUAD], I32)
        near = sb("near", [P, KV * QUAD])
        index = sb("index", [P, T, KV], U32)
        idle = sb("idle", [1, 2])
        gathered = sb("gathered", [P, 2, S * C])
        agg = sb("agg", [P, T, C])
        x_next = sb("x_next", [P, T, C])
        xc = sb("xc", [P, T, C])
        h = sb("h", [P, T, C])
        hT = sb("hT", [P, N])
        aggT = sb("aggT", [P, N])
        stats = sb("stats", [P, T, 6])
        meanvar_one = sb("meanvar_one", [P, T, 2])
        meanvar = sb("meanvar", [P, B, T, 2])
        var = sb("var", [P, B, T])
        root = sb("root", [P, B, T])
        rstd = sb("rstd", [P, B, T])
        shift = sb("shift", [P, B, T])
        wh = sb("wh", [P, T, C + 3 * HM])
        top_s2 = sb("top_s2", [P, HM])
        top_row = sb("top_row", [HM, 1])
        top_diag = sb("top_diag", [HM, HM])
        top_all = sb("top_all", [P, HM])
        s2_rel = sb("s2_rel", [P, T * HM])
        t_all = sb("t_all", [P, T * HM])
        t_neg = sb("t_neg", [P, T * HM])
        t_pos = sb("t_pos", [P, T * HM])
        s2_steep = sb("s2_steep", [P, T * HM])
        f1 = sb("f1", [P, T * HM])
        f2 = sb("f2", [P, T * HM])
        f2n = sb("f2n", [P, T * HM])
        e1 = sb("e1", [P, T * HM])
        e2 = sb("e2", [P, T * HM])
        cols = sb("cols", [P, T * 2 * (C + HM)])
        part = sb("part", [P, 3, T * 2 * (C + HM)], BF16)
        npart = sb("npart", [P, 3, T * (C + HM)], BF16)
        second = sb("second", [P, 2, C + 1])
        rden = sb("rden", [P, 2])
        numer = sb("numer", [P, 2, C + 1])
        y_pos = sb("y_pos", [P, C])
        y_neg = sb("y_neg", [P, 2, C])
        room = edges[:, :, :, :].bitcast(F32).rearrange("p h t n -> p (h t n)")
        x_all = room[:, 0:B * T * C].rearrange("p (b t c) -> p b t c", b=B, t=T)
        h_all = room[:, B * T * C:2 * B * T * C].rearrange("p (b t c) -> p b t c", b=B, t=T)
        w_turned = (hT[:, C:2 * C], hT[:, 2 * C:3 * C])

        ps_mask = ps("ps_mask", [P, T, P], BF16)
        ps_x = ps("ps_x", [P, 2, 512])
        ps_s = ps("ps_s", [P, 2, 512])
        ps_acc = ps("ps_acc", [P, 2, 512])
        ps_small = ps("ps_small", [P, 512])
        ps_code = ps_small[:, 512 - Q:512]
        ps_w = [ps_acc[:, 0, :], ps_acc[:, 1, :]]
        ps_wa = [ps_s[:, 0, :], ps_acc[:, 0, :], ps_acc[:, 1, :]]

        def s1_row(g):
            return (ps_s, ps_x)[g % 2][:, :, :]

        weights_in = sem("weights_in")
        consts_ready = sem("consts_ready")
        diag_ready = sem("diag_ready")
        wprep_ps = sem("wprep_ps")
        wprep_sb = sem("wprep_sb")
        weights_ready = sem("weights_ready")
        all_loaded = [sem("all_loaded0"), sem("all_loaded1")]
        x_loaded = sem("x_loaded")
        h0_loaded = sem("h0_loaded")
        table_stored = sem("table_stored")
        rows_stored = sem("rows_stored")
        adj_loaded = [sem("adj_loaded0"), sem("adj_loaded1")]
        gather_done = [sem("gather_done0"), sem("gather_done1")]
        chain_done = sem("chain_done")
        adj_cast = sem("adj_cast")
        mask_ps = sem("mask_ps")
        mask_next_ready = sem("mask_next_ready")
        mask_ready = sem("mask_ready")
        codes_ps = sem("codes_ps")
        codes_used = sem("codes_used")
        index_ready = sem("index_ready")
        idle_done = sem("idle_done")
        gather_free = sem("gather_free")
        norm_ready = sem("norm_ready")
        h_ready = sem("h_ready")
        turned_ps = sem("turned_ps")
        turned_sb = sem("turned_sb")
        sage_ps = sem("sage_ps")
        sage_used = sem("sage_used")
        wh_ps = sem("wh_ps")
        wh_sb = sem("wh_sb")
        s1_ps = sem("s1_ps")
        top_ready = sem("top_ready")
        top_turned = sem("top_turned")
        top_diag_ready = sem("top_diag_ready")
        top_spread = sem("top_spread")
        exp_in_ready = sem("exp_in_ready")
        exp_ready = sem("exp_ready")
        steep_ready = sem("steep_ready")
        cols_ready = sem("cols_ready")
        hi_ready = sem("hi_ready")
        rest_ready = sem("rest_ready")
        mid_ready = sem("mid_ready")
        lo_ready = sem("lo_ready")
        nparts_ready = sem("nparts_ready")
        rough_ready = sem("rough_ready")
        edges_ready = sem("edges_ready")
        acc_ready = sem("acc_ready")
        second_ready = sem("second_ready")
        acc_used = sem("acc_used")
        y_neg_ready = sem("y_neg_ready")
        elu_ready = sem("elu_ready")
        x_done = sem("x_done")

        block = ctx.enter_context(nc.Block())

        @block.sync
        def _(sp):
            def load(dst, src):
                sp.dma_start(dst, src, allow_slow_non_contiguous=True).then_inc(weights_in, 16)

            def load_adj(b, t):
                if not (isinstance(b, int) and b == 0 and t < 2):
                    sp.wait_ge(adj_cast, b * T + t - 1)
                sp.dma_start(adj_in[:, t % 2, :], adj_v[b, t]).then_inc(adj_loaded[t % 2], 16)

            def table_rows(b):
                return table_v[b, 0:N, :].rearrange("(t p) c -> p t c", p=P)

            def turn(b, more, more2):
                if more:
                    for t in range(2, T):
                        load_adj(b + 1, t)
                        if t == 3:
                            sp.wait_ge(sage_used, 2 * b + 2)
                            sp.dma_start(x_next[:, :, :], x_v[b + 1]).then_inc(x_loaded, 16)
                    if more2:
                        load_adj(b + 2, 0)
                        load_adj(b + 2, 1)
                    sp.wait_ge(turned_ps, 10 * (b + 1))
                    sp.dma_start(h[:, :, :], table_rows(b + 1)).then_inc(h0_loaded, 16)
                for half in range(2):
                    ts = slice(half * T // 2, (half + 1) * T // 2)
                    sp.wait_ge(x_done, 2 * b + half + 1)
                    sp.dma_start(out_v[b][:, ts, :], xc[:, ts, :]).then_inc(rows_stored, 16)

            for g in range(2):
                for b in range(g * B // 2, (g + 1) * B // 2):
                    sp.dma_start(x_all[:, b], x_v[b]).then_inc(all_loaded[g], 16)
                if g == 0:
                    load_adj(0, 0)
                    load_adj(0, 1)
            sp.wait_ge(consts_ready, 3)
            sp.dma_start(table_v[:, N, :], aggT[0:B, N - C:N]).then_inc(rows_stored, 16)
            load_adj(0, 2)
            load_adj(0, 3)
            for b in range(B):
                sp.wait_ge(h_ready, T * (b + 1))
                sp.dma_start(table_rows(b), h_all[:, b]).then_inc(table_stored, 16)
            load(w0_sb[:, :, :], w0.rearrange("(s k) o -> k s o", k=P))
            load(b0_row[:, :], b0.rearrange("(a n) -> a n", a=1))
            load(b2_row[:, 0:C], b2.rearrange("(a n) -> a n", a=1))
            load(b2_col[:, :], b2.rearrange("(n a) -> n a", a=1))
            load(wr[1][:, 0:C], w1)
            load(wr[3][:, 0:C], w3)
            load(hT[:, 0:C], w2)
            for l, a in ((1, a1), (3, a3)):
                for s in range(2):
                    load(aggT[:, 2 * l + s:2 * l + s + 1], a[s * C:(s + 1) * C, :])
            D = C // HM
            for s in range(2):
                for g in range(HM):
                    load(aggT[g * D:(g + 1) * D, 16 + s * HM + g:17 + s * HM + g],
                         a2[g, s * D:(s + 1) * D].rearrange("(d a) -> d a", a=1))
            sp.dma_start(x_next[:, :, :], x_v[0]).then_inc(x_loaded, 16)
            sp.wait_ge(table_stored, 16 * B)
            sp.dma_start(h[:, :, :], table_rows(0)).then_inc(h0_loaded, 16)
            for t in range(4, T):
                load_adj(0, t)
            load_adj(1, 0)
            load_adj(1, 1)
            with sp.Fori(0, B - 2) as b:
                turn(b, True, True)
            turn(B - 2, True, False)
            turn(B - 1, False, False)
            sp.wait_ge(rows_stored, 16 + 32 * B)

        @block.gpsimd
        def _(pool):
            nc.gpsimd.iota(code_base[:, :], pattern=[[-16, Q]], base=16 * Q, channel_multiplier=0,
                           allow_small_or_imprecise_dtypes=True).then_inc(diag_ready, 1)
            nc.gpsimd.memset(idle[:, :], 0.0).then_inc(diag_ready, 1)
            pool.wait_ge(diag_ready, 2)
            pool.wait_ge(consts_ready, 2)
            for m in (ident_bf, ident):
                nc.gpsimd.affine_select(out=m[:, :], in_=m[:, :], compare_op=ALU.not_equal, fill=1.0, base=0,
                                        pattern=[[-1, P]], channel_multiplier=1).then_inc(diag_ready, 1)
            nc.gpsimd.memset(quad_bits[:, :], 0.0).then_inc(diag_ready, 1)
            for k in range(QUAD):
                pool.wait_ge(diag_ready, 5 + k)
                nc.gpsimd.affine_select(out=quad_bits[:, :], in_=quad_bits[:, :], compare_op=ALU.not_equal,
                                        fill=float(8 >> k), base=-k, pattern=[[-QUAD, P // QUAD]],
                                        channel_multiplier=1).then_inc(diag_ready, 1)
            pool.wait_ge(rows_stored, 16)
            pool.wait_ge(table_stored, 16 * B)
            with pool.Fori(0, B) as b:
                for t in range(T):
                    pool.wait_ge(index_ready, b * T + t + 1)
                    nc.gpsimd.tensor_tensor(idle[:, 1:2], idle[:, 0:1], idle[:, 0:1], ALU.add)\
                      .then_inc(idle_done, 1)
                    pool.wait_ge(gather_free, 1)
                    pool.wait_ge(gather_free, b * T + t + 1)
                    pool.wait_ge(idle_done, b * T + t + 1)
                    for k in range(S):
                        nc.gpsimd.indirect_dma_start(
                            out=gathered[:, t % 2, k * C:(k + 1) * C], out_offset=None, in_=table,
                            in_offset=bass.IndirectOffsetOnAxis(ap=index[:, t, k:k + 1], axis=0),
                        ).then_inc(gather_done[t % 2], 16)

        @block.vector
        def _(dve):
            step = Chain(dve, chain_done)

            def row_stats(src, t):
                step(nc.vector.bn_stats(out=stats[:, t, :], in_=src[:, t, :]))

            def invert(bs):
                v, r, q = var[:, bs, :], rstd[:, bs, :], root[:, bs, :]
                step(nc.vector.tensor_scalar(v, meanvar[:, bs, :, 1], EPS, None, ALU.add))
                step.settle()
                step(nc.vector.tensor_scalar(q.bitcast(I32), v.bitcast(I32), 1, None, ALU.logical_shift_right))
                step.settle()
                step(nc.vector.tensor_scalar(r.bitcast(I32), q.bitcast(I32), -1.0, float(RSQRT_SEED),
                                             ALU.mult, ALU.add))
                step.settle()
                for _ in range(3):
                    step(nc.vector.tensor_tensor(q, r, r, ALU.mult))
                    step.settle()
                    step(nc.vector.scalar_tensor_tensor(out=q, in0=q, scalar=-0.5, in1=v,
                                                        op0=ALU.mult, op1=ALU.mult))
                    step.settle()
                    step(nc.vector.scalar_tensor_tensor(out=r, in0=q, scalar=1.5, in1=r,
                                                        op0=ALU.add, op1=ALU.mult))
                    step.settle()
                nc.vector.scalar_tensor_tensor(out=shift[:, bs, :], in0=meanvar[:, bs, :, 0], scalar=-1.0, in1=r,
                                               op0=ALU.mult, op1=ALU.mult).then_inc(norm_ready, 1)

            def norm():
                step.settle()
                for t in range(T):
                    step(nc.vector.bn_aggr(out=meanvar[:, 0, t, :], in_=stats[:, t, :]))
                step.settle()
                invert(slice(0, 1))

            def eight_largest(src):
                for r in range(KV // 8):
                    eight = top[:, 8 * r:8 * r + 8]
                    step(nc.vector.max(out=eight, in_=src[:, :]))
                    step.settle()
                    if r < KV // 8 - 1:
                        step(nc.vector.match_replace(out=src[:, :], in_to_replace=eight, in_values=src[:, :],
                                                     imm_value=0.0))
                        step.settle()

            def first_quads(b, t):
                dve.wait_ge(codes_ps, b * T + t + 1)
                step(nc.vector.scalar_tensor_tensor(out=codes[:, :], in0=ps_code, scalar=0.0, in1=code_base[:, :],
                                                    op0=ALU.is_gt, op1=ALU.mult))
                step.settle()
                step(nc.vector.tensor_tensor(codes[:, :], codes[:, :], ps_code, ALU.add))
                step.settle()
                eight_largest(codes)
                nc.vector.tensor_copy(top_int[:, :], top[:, :]).then_inc(codes_used, 1)

            def first_neighbours(b, t):
                dve.wait_ge(codes_used, b * T + t + 1)
                step(nc.vector.tensor_scalar(quad_up[:, :], top_int[:, :], 4, None, ALU.logical_shift_right))
                step(nc.vector.tensor_tensor(bits[:, :, :], top_int[:, :].unsqueeze(2).to_broadcast([P, KV, QUAD]),
                                             bit_of[:, :].unsqueeze(1).to_broadcast([P, KV, QUAD]), ALU.bitwise_and))
                step.settle()
                near_v = near[:, :].rearrange("p (k q) -> p k q", q=QUAD)
                step(nc.vector.scalar_tensor_tensor(
                    out=near_v, in0=quad_up[:, :].unsqueeze(2).to_broadcast([P, KV, QUAD]), scalar=float(QUAD),
                    in1=place[:, :].unsqueeze(1).to_broadcast([P, KV, QUAD]), op0=ALU.mult, op1=ALU.subtract))
                step.settle()
                step(nc.vector.scalar_tensor_tensor(out=near_v, in0=bits[:, :, :], scalar=0.0, in1=near_v,
                                                    op0=ALU.is_gt, op1=ALU.mult))
                step.settle()
                eight_largest(near)
                nc.vector.tensor_scalar(index[:, t, :], top[:, :], -1.0, first_row[:, 0:1],
                                        ALU.mult, ALU.add).then_inc(index_ready, 1)

            def list_neighbours(b, t):
                first_quads(b, t)
                first_neighbours(b, t)

            def next_rows():
                step.settle()
                step(nc.vector.tensor_scalar(first_row[:, :], first_row[:, :], float(ROWS), None, ALU.add))
                step.settle()

            def take_maximum(b, t):
                dve.wait_ge(gather_done[t % 2], b * (16 * S * T // 2) + 16 * S * (t // 2 + 1))
                nc.vector.tensor_reduce(agg[:, t, :], gathered[:, t % 2, :].rearrange("p (k c) -> p c k", k=S),
                                        AX.X, ALU.max).then_inc(gather_free, 1)

            def beside(b, layer, i):
                if (layer, i) in MAXIMA:
                    take_maximum(b + 1, MAXIMA[layer, i])
                for t, second_part in LISTS.get((layer, i), []):
                    (first_neighbours if second_part else first_quads)(b + 1, t)

            def attention(b, layer, more):
                H, D1 = HEADS[layer], width(layer)
                D = D1 - 1
                HT = T * H
                m = b * 3 + (layer - 1)
                s1 = wh[:, :, C:C + H]
                s2 = wh[:, :, C + H:C + 2 * H]
                minus_s2 = wh[:, :, C + 2 * H:C + 3 * H]

                def small(tile):
                    return tile[:, 0:HT].rearrange("p (t h) -> p t h", h=H)

                def mark_edges(g, tiles):
                    k = G0[layer] + g
                    if shared(k):
                        for t in tiles:
                            dve.wait_ge(rough_ready, b * ((NG - 1) * T) + rough_count(k, t))
                            nc.vector.tensor_tensor(edges[:, g, t, :], edges[:, g, t, :], mask[:, t, :], ALU.min)\
                              .then_inc(edges_ready, 1)
                    else:
                        dve.wait_ge(s1_ps, b * NG + k + 1)
                        for t in tiles:
                            nc.vector.scalar_tensor_tensor(
                                out=edges[:, g, t, :], in0=s1_row(k).rearrange("p a n -> p (a n)"),
                                scalar=minus_s2[:, t, g:g + 1], in1=mask[:, t, :],
                                op0=ALU.is_gt, op1=ALU.mult).then_inc(edges_ready, 1)

                for t in range(T):
                    dve.wait_ge(wh_ps, b * 24 + 8 * (layer - 1) + t + 1)
                    nc.vector.tensor_copy(wh[:, t, 0:C + 3 * H], ps_w[t % 2][:, 0:C + 3 * H]).then_inc(wh_sb, 1)
                dve.wait_ge(wh_sb, b * 24 + 8 * layer)
                nc.vector.tensor_reduce(top_s2[:, 0:H], s2.rearrange("p t h -> p h t"), AX.X, ALU.max)\
                  .then_inc(top_ready, 1)
                nc.vector.tensor_scalar(small(s2_steep), minus_s2, -STEEP, None, ALU.mult).then_inc(steep_ready, 1)
                dve.wait_ge(top_turned, m + 1)
                step(nc.vector.tensor_reduce(top_row[0:H, :], ps_small[0:H, 0:P], AX.X, ALU.max))
                step.settle()
                nc.vector.tensor_scalar(top_diag[0:H, 0:H], ident[0:H, 0:H], top_row[0:H, 0:1], None, ALU.mult)\
                  .then_inc(top_diag_ready, 1)
                dve.wait_ge(top_spread, m + 1)
                step(nc.vector.tensor_copy(top_all[:, 0:H], ps_small[:, 0:H]))
                step.settle()
                spread = top_all[:, 0:H].unsqueeze(1).to_broadcast([P, T, H])
                step(nc.vector.tensor_tensor(small(s2_rel), s2, spread, ALU.subtract))
                step(nc.vector.tensor_tensor(small(t_all), s1, spread, ALU.add))
                step.settle()
                nc.vector.tensor_scalar(t_neg[:, 0:HT], t_all[:, 0:HT], 0.0, None, ALU.min).then_inc(exp_in_ready, 1)
                nc.vector.tensor_scalar(t_pos[:, 0:HT], t_all[:, 0:HT], 0.0, None, ALU.max).then_inc(exp_in_ready, 1)
                dve.wait_ge(exp_ready, 2 * m + 1)
                step(nc.vector.tensor_scalar(f2n[:, 0:HT], f2[:, 0:HT], -1.0, None, ALU.mult))
                step.settle()
                cv = cols[:, 0:HT * 2 * D1].rearrange("p (t h s d) -> p t h s d", h=H, s=2, d=D1)
                whv = wh[:, :, 0:C].rearrange("p t (h d) -> p t h d", d=D)
                W = TC * H * 2 * D1
                for c in range(CH):
                    ts = slice(c * TC, (c + 1) * TC)
                    for s, f in enumerate((f1, f2n)):
                        step(nc.vector.tensor_tensor(cv[:, ts, :, s, 0:D], whv[:, ts],
                                                     small(f)[:, ts].unsqueeze(3).to_broadcast([P, TC, H, D]),
                                                     ALU.mult))
                        ins = nc.vector.tensor_copy(cv[:, ts, :, s, D], small(f)[:, ts])
                        if s:
                            ins.then_inc(cols_ready, 1)
                        else:
                            step(ins)
                step.settle()
                for c in range(CH):
                    dve.wait_ge(hi_ready, b * (3 * CH) + CH * (layer - 1) + c + 1)
                    nc.vector.tensor_tensor(cols[:, c * W:(c + 1) * W], cols[:, c * W:(c + 1) * W],
                                            part[:, 0, c * W:(c + 1) * W], ALU.subtract).then_inc(rest_ready, 1)
                if layer == 2:
                    mark_edges(0, range(0, 1))
                for c in range(CH):
                    dve.wait_ge(mid_ready, b * (3 * CH) + CH * (layer - 1) + c + 1)
                    dve.wait_ge(rest_ready, b * (3 * CH) + CH * (layer - 1) + c + 1)
                    step(nc.vector.tensor_tensor(part[:, 2, c * W:(c + 1) * W], cols[:, c * W:(c + 1) * W],
                                                 part[:, 1, c * W:(c + 1) * W], ALU.subtract))
                    step.settle()
                    nc.vector.tensor_scalar(
                        npart[:, :, c * W // 2:(c + 1) * W // 2].rearrange("p k (q d) -> p k q d", d=D1),
                        part[:, :, c * W:(c + 1) * W].rearrange("p k (q s d) -> p k q s d", s=2, d=D1)[:, :, :, 1, :],
                        -1.0, None, ALU.mult).then_inc(nparts_ready, 1)
                mark_edges(0, range(int(layer == 2), T))
                HG = H // GROUPS[layer]
                for g in range(1, HG):
                    mark_edges(g, range(T))

                for i in range(GROUPS[layer] * T):
                    t, g0 = i % T, i // T * HG
                    if more:
                        beside(b, layer, i)
                    for g, j in second_group(layer, i - 1):
                        mark_edges(g, [j])
                    n = b * NA + A0[layer] + i
                    dve.wait_ge(second_ready, n + 1)
                    acc = ps_acc[:, i % 2, 0:2 * HG * D1].rearrange("p (h s d) -> p h s d", h=HG, s=2)
                    for g in range(HG):
                        at = t * H + g0 + g
                        ins = nc.vector.scalar_tensor_tensor(
                            out=numer[:, i % 2, g * D1:(g + 1) * D1], in0=acc[:, g, 0, :], scalar=e1[:, at:at + 1],
                            in1=second[:, i % 2, g * D1:(g + 1) * D1], op0=ALU.mult, op1=ALU.add)
                        if g < HG - 1:
                            step(ins)
                        else:
                            ins.then_inc(acc_used, 1)
                    dve.wait_ge(acc_used, n + 1)
                    nv = numer[:, i % 2, 0:HG * D1].rearrange("p (h d) -> p h d", d=D1)
                    step.settle()
                    step(nc.vector.reciprocal(rden[:, 0:HG], nv[:, :, D]))
                    step.settle()
                    if layer == 1:
                        if i:
                            add_elu(b, i - 1)
                        nc.vector.tensor_scalar(y_neg[:, i % 2, :], numer[:, i % 2, 0:D], rden[:, 0:1], 0.0,
                                                ALU.mult, ALU.min).then_inc(y_neg_ready, 1)
                        step(nc.vector.tensor_scalar(y_pos[:, :], numer[:, i % 2, 0:D], rden[:, 0:1], 0.0,
                                                     ALU.mult, ALU.max))
                        step.settle()
                        step(nc.vector.tensor_tensor(xc[:, t, :], xc[:, t, :], y_pos[:, :], ALU.add))
                        if i:
                            row_stats(xc, i - 1)
                    else:
                        for g in range(HG):
                            xs = xc[:, t, (g0 + g) * D:(g0 + g + 1) * D]
                            ins = nc.vector.scalar_tensor_tensor(
                                out=xs, in0=numer[:, i % 2, g * D1:g * D1 + D], scalar=rden[:, g:g + 1], in1=xs,
                                op0=ALU.mult, op1=ALU.add)
                            if layer == 3 and i % (T // 2) == T // 2 - 1:
                                ins.then_inc(x_done, 1)
                            else:
                                step(ins)
                        if layer == 2 and g0 + HG == H:
                            step.settle()
                            row_stats(xc, t)
                if layer == 1:
                    add_elu(b, T - 1)
                    row_stats(xc, T - 1)

            def add_elu(b, t):
                dve.wait_ge(elu_ready, b * T + t + 1)
                step.settle()
                step(nc.vector.scalar_tensor_tensor(out=xc[:, t, :], in0=y_neg[:, t % 2, :], scalar=-1.0,
                                                    in1=xc[:, t, :], op0=ALU.add, op1=ALU.add))
                step.settle()

            def turn(b, more):
                take_maximum(b, T - 1)
                if more:
                    next_rows()
                    first_quads(b + 1, 0)
                dve.wait_ge(x_loaded, b * 16 + 16)
                dve.wait_ge(rows_stored, b * 32 + 16)
                for half in range(2):
                    ts = slice(half * 4, half * 4 + 4)
                    dve.wait_ge(sage_ps, 2 * b + half + 1)
                    nc.vector.scalar_tensor_tensor(
                        out=xc[:, ts, :], in0=ps_s[:, half, :].rearrange("p (t c) -> p t c", c=C), scalar=0.0,
                        in1=x_next[:, ts, :], op0=ALU.max, op1=ALU.add).then_inc(sage_used, 1)
                    dve.wait_ge(sage_used, 2 * b + half + 1)
                    for t in range(half * 4, half * 4 + 4):
                        row_stats(xc, t)
                for layer in (1, 2, 3):
                    norm()
                    if more:
                        beside(b, layer, -1)
                    attention(b, layer, more)

            nc.vector.memset(ident[:, :], 0.0).then_inc(consts_ready, 1)
            nc.vector.memset(ident_bf[:, :], 0.0).then_inc(consts_ready, 1)
            nc.vector.memset(aggT[:, 16:N], 0.0).then_inc(consts_ready, 1)
            nc.vector.memset(first_row[:, :], float(N)).then_inc(gather_free, 2)
            step(nc.vector.memset(ones[:, :], 1.0))
            for k in range(QUAD):
                step(nc.vector.memset(bit_of[:, k:k + 1], 8 >> k))
                step(nc.vector.memset(place[:, k:k + 1], float(k)))
            step.restart()
            for g in range(2):
                dve.wait_ge(all_loaded[g], 16 * (B // 2))
                with dve.Fori(g * B // 2, (g + 1) * B // 2) as b:
                    for t in range(T):
                        step(nc.vector.bn_stats(out=stats[:, t, :], in_=x_all[:, b, t, :]))
                    step.settle()
                    for t in range(T):
                        step(nc.vector.bn_aggr(out=meanvar_one[:, t, :], in_=stats[:, t, :]))
                    step.settle()
                    step(nc.vector.tensor_copy(meanvar[:, b, :, :], meanvar_one[:, :, :]))
                    step.restart()
                invert(slice(g * B // 2, (g + 1) * B // 2))
                step.restart()
            dve.wait_ge(diag_ready, 1)
            dve.wait_ge(gather_free, 2)
            list_neighbours(0, 0)
            list_neighbours(0, 1)
            for n, l in enumerate((1, 3, 2)):
                H = HEADS[l]
                if l == 2:
                    dve.wait_ge(wprep_ps, 5)
                    step(nc.vector.tensor_copy(wr[2][:, 0:C], ps_x[:, 0, 0:C]))
                    step(nc.vector.tensor_copy(b2_row[:, C:C + 2 * H], ps_wa[2][0:1, 64:64 + 2 * H]))
                    step.settle()
                    step(nc.vector.scalar_tensor_tensor(
                        out=b2_row[:, C + 2 * H:C + 3 * H], in0=b2_row[:, C:C + H], scalar=-1.0,
                        in1=b2_row[:, C + H:C + 2 * H], op0=ALU.mult, op1=ALU.subtract))
                else:
                    dve.wait_ge(wprep_ps, 2 * n + 1)
                    nc.vector.tensor_copy(w_turned[n], ps_x[:, n, 0:C]).then_inc(wprep_sb, 1)
                    dve.wait_ge(wprep_ps, 2 * n + 2)
                step(nc.vector.tensor_copy(wr[l][:, C:C + 2 * H], ps_wa[n][:, 0:2 * H]))
                step(nc.vector.tensor_scalar(wr[l][:, C + 2 * H:C + 3 * H], ps_wa[n][:, H:2 * H],
                                             -1.0, None, ALU.mult))
                step.settle()
                for g in range(H):
                    nc.vector.tensor_scalar(wa1[l][:, g, :], ones[:, :], wr[l][:, C + g:C + g + 1], None,
                                            ALU.mult).then_inc(weights_ready, 1)
            list_neighbours(0, 2)
            list_neighbours(0, 3)
            for t in range(4, T):
                take_maximum(0, t - 4)
                list_neighbours(0, t)
            for t in range(T - 4, T - 1):
                take_maximum(0, t)
            step.restart()
            with dve.Fori(0, B - 1) as b:
                turn(b, True)
                step.restart()
            turn(B - 1, False)

        @block.scalar
        def _(act):
            def norm(src, dst, k, tiles):
                for t in tiles:
                    nc.scalar.activation(dst[:, t, :], src[:, t, :], ACT.Relu, bias=shift[:, k, t:t + 1],
                                         scale=rstd[:, k, t:t + 1]).then_inc(h_ready, 1)

            def cast_mask(b, t):
                n = b * T + t
                act.wait_ge(adj_loaded[t % 2], b * (16 * T // 2) + 16 * (t // 2 + 1))
                if not (isinstance(b, int) and b == 0 and t < 2):
                    act.wait_ge(mask_ps, n - 1)
                nc.scalar.activation(adj_bf[:, t % 2, :], adj_in[:, t % 2, :], ACT.Copy).then_inc(adj_cast, 1)

            def keep_mask(b, t):
                act.wait_ge(mask_ps, b * T + t + 1)
                if t == 0 and not (isinstance(b, int) and b == 0):
                    act.wait_ge(mask_ready, b * T)
                nc.scalar.activation(mask_next[:, :, t * P:(t + 1) * P], ps_mask[:, :, :], ACT.Copy)\
                  .then_inc(mask_next_ready, 1)

            def keep_and_cast(b, t, more2):
                keep_mask(b + 1, t)
                if t + 2 < T:
                    cast_mask(b + 1, t + 2)
                elif more2:
                    cast_mask(b + 2, t + 2 - T)

            def bring_forward(b, t):
                nc.scalar.activation(mask[:, :, t * P:(t + 1) * P], mask_next[:, :, t * P:(t + 1) * P], ACT.Copy)\
                  .then_inc(mask_ready, 1)

            def keep_turned(b, s, half, dst):
                act.wait_ge(turned_ps, b * 10 + 2 * s + half + 1)
                nc.scalar.activation(dst[:, half * 512:(half + 1) * 512], ps_x[:, half, :], ACT.Copy)\
                  .then_inc(turned_sb, 1)

            def rough_edges(b, k, tiles):
                layer = max(l for l in (1, 2, 3) if k >= G0[l])
                g = k - G0[layer]
                act.wait_ge(s1_ps, b * NG + k + 1)
                for t in tiles:
                    at = t * HEADS[layer] + g
                    nc.scalar.activation(edges[:, g, t, :], s1_row(k).rearrange("p a n -> p (a n)"), ACT.Relu,
                                         bias=s2_steep[:, at:at + 1], scale=STEEP).then_inc(rough_ready, 1)

            def attention(b, layer):
                H, D1 = HEADS[layer], width(layer)
                HT = T * H
                W = TC * H * 2 * D1
                act.wait_ge(norm_ready, b * 3 + 2 + layer)
                norm(xc, h, 0, range(0, 6))
                keep_turned(b, layer + 1, 0, hT)
                norm(xc, h, 0, range(6, T))
                keep_turned(b, layer + 1, 1, hT)
                act.wait_ge(steep_ready, b * 3 + layer)
                act.wait_ge(exp_in_ready, b * 6 + 2 * layer)
                nc.scalar.activation(f1[:, 0:HT], s2_rel[:, 0:HT], ACT.Exp)
                nc.scalar.activation(f2[:, 0:HT], s2_rel[:, 0:HT], ACT.Exp, scale=SLOPE)\
                  .then_inc(exp_ready, 1)
                nc.scalar.activation(e1[:, 0:HT], t_neg[:, 0:HT], ACT.Exp, scale=1.0 - SLOPE)
                nc.scalar.activation(e2[:, 0:HT], t_pos[:, 0:HT], ACT.Exp, scale=SLOPE - 1.0)\
                  .then_inc(exp_ready, 1)
                for c in range(CH):
                    act.wait_ge(cols_ready, b * (3 * CH) + CH * (layer - 1) + c + 1)
                    nc.scalar.activation(part[:, 0, c * W:(c + 1) * W], cols[:, c * W:(c + 1) * W], ACT.Copy)\
                      .then_inc(hi_ready, 1)
                first = G0[layer] + (layer == 2)
                rough_edges(b, first, [0])
                for c in range(CH):
                    act.wait_ge(rest_ready, b * (3 * CH) + CH * (layer - 1) + c + 1)
                    nc.scalar.activation(part[:, 1, c * W:(c + 1) * W], cols[:, c * W:(c + 1) * W], ACT.Copy)\
                      .then_inc(mid_ready, 1)
                rough_edges(b, first, range(1, T))

            def second_half(b, layer, i):
                H, D1 = HEADS[layer], width(layer)
                HG = H // GROUPS[layer]
                t, g0 = i % T, i // T * HG
                n = b * NA + A0[layer] + i
                act.wait_ge(acc_ready, n + 1)
                if i >= 2:
                    act.wait_ge(acc_used, n - 1)
                acc = ps_acc[:, i % 2, 0:2 * HG * D1].rearrange("p (h s d) -> p h s d", h=HG, s=2)
                for g in range(HG):
                    at = t * H + g0 + g
                    ins = nc.scalar.activation(second[:, i % 2, g * D1:(g + 1) * D1], acc[:, g, 1, :],
                                               ACT.Copy, scale=e2[:, at:at + 1])
                ins.then_inc(second_ready, 1)

            def elu_exp(b, t):
                act.wait_ge(y_neg_ready, b * T + t + 1)
                nc.scalar.activation(y_neg[:, t % 2, :], y_neg[:, t % 2, :], ACT.Exp).then_inc(elu_ready, 1)

            def turn(b, more, more2):
                if more:
                    keep_and_cast(b, 0, more2)
                keep_turned(b, 1, 1, aggT)
                if more:
                    keep_and_cast(b, 1, more2)
                for layer in (1, 2, 3):
                    attention(b, layer)
                    for i in range(GROUPS[layer] * T):
                        if more and (layer, i) in TURNS:
                            keep_and_cast(b, TURNS[layer, i], more2)
                        for g, j in second_group(layer, i):
                            rough_edges(b, G0[2] + g, [j])
                        second_half(b, layer, i)
                        if layer == 1 and i:
                            elu_exp(b, i - 1)
                        if more and layer == 3:
                            if i == 0:
                                act.wait_ge(mask_next_ready, b * T + 2 * T)
                            bring_forward(b + 1, i)
                            if i in H0_TURNS:
                                keep_turned(b + 1, *divmod(H0_TURNS.index(i), 2), (hT, hT, aggT)[H0_TURNS.index(i)])
                    if layer == 1:
                        elu_exp(b, T - 1)

            cast_mask(0, 0)
            cast_mask(0, 1)
            keep_mask(0, 0)
            cast_mask(0, 2)
            keep_mask(0, 1)
            cast_mask(0, 3)
            for g in range(2):
                act.wait_ge(norm_ready, g + 1)
                with act.Fori(g * B // 2, (g + 1) * B // 2) as b:
                    norm(x_all[:, b], h_all[:, b], b, range(T))
            for t in range(2, T):
                keep_mask(0, t)
                cast_mask((t + 2) // T, (t + 2) % T)
            act.wait_ge(mask_next_ready, T)
            for t in range(T):
                bring_forward(0, t)
            for half in range(2):
                keep_turned(0, 0, half, hT)
            keep_turned(0, 1, 0, aggT)
            with act.Fori(0, B - 2) as b:
                turn(b, True, True)
            turn(B - 2, True, False)
            turn(B - 1, False, False)

        @block.tensor
        def _(pe):
            def turn_mask(b, t):
                n = b * T + t
                pe.wait_ge(adj_cast, n + 1)
                if not (isinstance(b, int) and n == 0):
                    pe.wait_ge(mask_next_ready, n)
                for j in range(T):
                    ins = nc.tensor.transpose(ps_mask[:, j, :], adj_bf[:, t % 2, j * P:(j + 1) * P], ident_bf[:, :])
                ins.then_inc(mask_ps, 1)

            def make_codes(b, t):
                n = b * T + t
                pe.wait_ge(mask_next_ready, n + 1)
                if not (isinstance(b, int) and n == 0):
                    pe.wait_ge(codes_used, n)
                for j in range(T):
                    ins = nc.tensor.matmul(ps_code[:, j * (P // QUAD):(j + 1) * (P // QUAD)],
                                           mask_next[:, j, t * P:(t + 1) * P], quad_bits[:, :],
                                           start=True, stop=True)
                ins.then_inc(codes_ps, 1)

            def turn_features(b, s, half, src, norms=None):
                if s:
                    pe.wait_ge(turned_sb, b * 10 + 2 * s + half - 1)
                for t in range(4 * half, 4 * half + 4):
                    if norms is not None:
                        pe.wait_ge(h_ready, norms + t + 1)
                    ins = nc.tensor.transpose(ps_x[:, half, t % 4 * P:(t % 4 + 1) * P], src[:, t, :], ident[:, :])
                ins.then_inc(turned_ps, 1)

            def turn_early(b, k):
                if k == 0:
                    pe.wait_ge(h0_loaded, b * 16 + 16)
                if k == 2:
                    pe.wait_ge(gather_free, b * T + T // 2 + 2)
                turn_features(b, k // 2, k % 2, (h, h, agg)[k])

            def sage_part(s, t, src, start, stop):
                o = ps_s[:, t // 4, t % 4 * P:(t % 4 + 1) * P]
                return nc.tensor.matmul(o, src[:, t * P:(t + 1) * P], w0_sb[:, s, :], start=start, stop=stop,
                                        skip_group_check=True)

            def sage_h(b):
                pe.wait_ge(turned_sb, b * 10 + 2)
                for t in range(T):
                    sage_part(0, t, hT, start=(t % 4 == 0), stop=False)
                    nc.tensor.matmul(ps_s[:, t // 4, t % 4 * P:(t % 4 + 1) * P], ones[0:1, :], b0_row[:, :],
                                     start=False, stop=False, skip_group_check=True)

            def sage(b):
                pe.wait_ge(gather_free, b * T + T + 2)
                turn_features(b, 1, 1, agg)
                for half in range(2):
                    pe.wait_ge(turned_sb, b * 10 + 3 + half)
                    for t in range(4 * half, 4 * half + 4):
                        ins = sage_part(1, t, aggT, start=False, stop=(t % 4 == 3))
                    ins.then_inc(sage_ps, 1)

            def attention(b, layer, more):
                H, D1 = HEADS[layer], width(layer)
                m = b * 3 + (layer - 1)
                WW = C + 3 * H

                def spread_s1(g):
                    k = G0[layer] + g
                    for half in range(2):
                        ins = nc.tensor.matmul(s1_row(k)[:, half, :], wa1[layer][:, g, :],
                                               hT[:, half * 512:(half + 1) * 512], start=True, stop=True)
                    ins.then_inc(s1_ps, 1)

                for half in range(2):
                    turn_features(b, layer + 1, half, h, b * (3 * T) + (B + layer - 1) * T)
                for t in range(T):
                    n = b * 24 + 8 * (layer - 1) + t
                    if t % 4 == 0:
                        pe.wait_ge(turned_sb, b * 10 + 2 * layer + 3 + t // 4)
                    if t >= 2:
                        pe.wait_ge(wh_sb, n - 1)
                    o = ps_w[t % 2][:, 0:WW]
                    ins = nc.tensor.matmul(o, hT[:, t * P:(t + 1) * P], wr[layer][:, :], start=True, stop=layer != 2)
                    if layer == 2:
                        ins = nc.tensor.matmul(o, ones[0:1, :], b2_row[:, 0:WW], start=False, stop=True)
                    ins.then_inc(wh_ps, 1)
                pe.wait_ge(top_ready, m + 1)
                nc.tensor.transpose(ps_small[0:H, 0:P], top_s2[:, 0:H], ident[:, :]).then_inc(top_turned, 1)
                pe.wait_ge(top_diag_ready, m + 1)
                nc.tensor.matmul(ps_small[:, 0:H], ones[0:H, :], top_diag[0:H, 0:H], start=True, stop=True)\
                  .then_inc(top_spread, 1)
                for g in range(min(H, 2)):
                    spread_s1(g)
                WJ = 2 * H * D1
                HG = H // GROUPS[layer]
                for i in range(GROUPS[layer] * T):
                    if more and (layer, i) in CODES:
                        if i == 0:
                            pe.wait_ge(exp_in_ready, b * 6 + 2 * layer)
                        make_codes(b + 1, CODES[layer, i])
                    if more and (layer, i) in TURNS:
                        turn_mask(b + 1, TURNS[layer, i])
                    if layer == 2 and i == 1:
                        pe.wait_ge(edges_ready, b * (NG * T) + (G0[layer] + 1) * T)
                        spread_s1(2)
                        pe.wait_ge(rough_ready, b * ((NG - 1) * T) + rough_count(G0[2] + 1, T - 1))
                        spread_s1(3)
                    if more and layer == 3 and i in H0_TURNS:
                        turn_early(b + 1, H0_TURNS.index(i))
                    if more and layer == 3 and i == H0_PRODUCTS:
                        sage_h(b + 1)
                    t, g0 = i % T, i // T * HG
                    n = b * NA + A0[layer] + i
                    if i >= 2:
                        pe.wait_ge(acc_used, n - 1)
                    acc = ps_acc[:, i % 2, 0:2 * HG * D1]
                    acc_v = acc.rearrange("p (h s d) -> p h s d", h=HG, s=2)
                    for j in range(T):
                        if i == 0 and j % TC == 0:
                            pe.wait_ge(nparts_ready, b * (3 * CH) + CH * (layer - 1) + j // TC + 1)
                        if t == 0:
                            pe.wait_ge(edges_ready, b * (NG * T) + (G0[layer] + g0 + HG - 1) * T + j + 1)
                        for g in range(HG):
                            for k in range(3):
                                at = j * WJ + (g0 + g) * 2 * D1
                                nc.tensor.matmul(acc[:, g * 2 * D1:(g + 1) * 2 * D1],
                                                 edges[:, g0 + g, j, t * P:(t + 1) * P], part[:, k, at:at + 2 * D1],
                                                 start=(j == g == k == 0), stop=False, skip_group_check=True)
                        for k in range(3):
                            at = j * (WJ // 2) + g0 * D1
                            ins = nc.tensor.matmul(acc_v[:, :, 1, :], mask[:, j, t * P:(t + 1) * P],
                                                   npart[:, k, at:at + HG * D1].rearrange("p (h d) -> p h d", h=HG),
                                                   start=False, stop=(j == T - 1 and k == 2), skip_group_check=True)
                    ins.then_inc(acc_ready, 1)

            def turn(b, more, more2):
                if more:
                    make_codes(b + 1, 0)
                sage(b)
                if more:
                    turn_mask(b + 1, 1)
                for layer in (1, 2, 3):
                    attention(b, layer, more)
                if more2:
                    turn_mask(b + 2, 0)

            pe.wait_ge(diag_ready, 9)
            for t in range(2):
                turn_mask(0, t)
                make_codes(0, t)
            pe.wait_ge(weights_in, 16 * (11 + 2 * HM))
            for n, l in enumerate((1, 3)):
                nc.tensor.transpose(ps_x[:, n, 0:C], wr[l][:, 0:C], ident[:, :]).then_inc(wprep_ps, 1)
                pe.wait_ge(wprep_sb, n + 1)
                nc.tensor.matmul(ps_wa[n][:, 0:2], w_turned[n], aggT[:, 2 * l:2 * l + 2],
                                 start=True, stop=True).then_inc(wprep_ps, 1)
            block_diag = aggT[:, 16:16 + 2 * HM]
            nc.tensor.matmul(ps_wa[2][:, 0:2 * HM], hT[:, 0:C], block_diag, start=True, stop=True)
            nc.tensor.matmul(ps_wa[2][0:1, 64:64 + 2 * HM], b2_col[:, 0:1], block_diag, start=True, stop=True)
            pe.wait_ge(wprep_sb, 1)
            nc.tensor.transpose(ps_x[:, 0, 0:C], hT[:, 0:C], ident[:, :]).then_inc(wprep_ps, 1)
            for t in range(2, T):
                turn_mask(0, t)
                make_codes(0, t)
            turn_mask(1, 0)
            pe.wait_ge(weights_ready, NG)
            for k in range(3):
                turn_early(0, k)
            sage_h(0)
            with pe.Fori(0, B - 2) as b:
                turn(b, True, True)
            turn(B - 2, True, False)
            turn(B - 1, False, False)


_INS = ['x', 'adj', 'L0_gnn_W', 'L0_gnn_b', 'L1_gnn_W', 'L1_gnn_a', 'L2_gnn_W', 'L2_gnn_b', 'L2_gnn_a', 'L3_gnn_W',
        'L3_gnn_a']
_OUTS = [((8, 1024, 128), 'float32')]


def kernel(**inputs):
    import numpy as _np
    import concourse.bacc as _bacc
    from concourse import mybir as _mybir
    from concourse.bass_utils import run_bass_kernel_spmd as _run

    nc = _bacc.Bacc("TRN2", target_bir_lowering=False, num_devices=1)
    arrays, args = {}, []
    for name in _INS:
        a = _np.ascontiguousarray(inputs[name])
        arrays[f"in_{name}_dram"] = a
        args.append(nc.dram_tensor(f"in_{name}_dram", a.shape, _mybir.dt.from_np(a.dtype), kind="ExternalInput").ap())
    for i, (shape, dtype) in enumerate(_OUTS):
        dt = _mybir.dt.from_np(_np.dtype(dtype))
        args.append(nc.dram_tensor(f"out_{i}_dram", shape, dt, kind="ExternalOutput").ap())
    graph_layers(nc, *args)
    r = _run(nc, [arrays], core_ids=[0])
    got = tuple(r.results[0][f"out_{i}_dram"] for i in range(len(_OUTS)))
    return got[0]
```

```python
from contextlib import ExitStack

import concourse.bass as bass
from concourse import mybir

P = 128
F32 = mybir.dt.float32
BF16 = mybir.dt.bfloat16
I32 = mybir.dt.int32
U32 = mybir.dt.uint32
ALU = mybir.AluOpType
ACT = mybir.ActivationFunctionType
AX = mybir.AxisListType

S = 25
EPS = 1e-5
SLOPE = 0.2
RSQRT_SEED = 0x5F3759DF
STEEP = 2.0 ** 64


class Chain:

    def __init__(self, eng, sem):
        self.eng, self.sem, self.n = eng, sem, 0

    def __call__(self, ins):
        self.n += 1
        return ins.then_inc(self.sem, 1)

    def settle(self, n=None):
        self.eng.wait_ge(self.sem, self.n if n is None else n)

    def restart(self):
        self.settle()
        self.eng.sem_clear(self.sem)
        self.n = 0


def graph_layers(nc, x, adj, w0, b0, w1, a1, w2, b2, a2, w3, a3, out):
    B, N, C = x.shape
    T = N // P
    HEADS = [0, 1, a2.shape[0], 1]
    HM = max(HEADS)
    G0 = [0, 0, 1, 1 + HM]
    NG = sum(HEADS)
    GROUPS = [0, 1, 2, 1]
    A0 = [0, 0, T, 3 * T]
    NA = 4 * T
    QUAD = 4
    Q = N // QUAD
    KV = 8 * ((S + 7) // 8)
    SLOTS = 3
    ROWS = N + 1
    CH = 2
    TC = T // CH
    assert C == P and N % P == 0 and T == 8 and HM == 4 and B % 2 == 0

    H0_TURNS = (4, 6)

    def width(layer):
        return C // HEADS[layer] + 1

    def second_group(layer, i):
        if layer != 2 or not -1 <= i < T - 1:
            return []
        return [(HM // 2 + q // T, q % T) for q in range(2 * i + 3 if i >= 0 else 0, min(2 * i + 5, 2 * T))]

    ALONE = T // 2

    def shared(k, t):
        return k != G0[2] or t < ALONE

    def rough_count(k, t):
        return k * T - (k > G0[2]) * (T - ALONE) + t + 1

    NR = rough_count(NG - 1, T - 1)

    LISTS = {
        (1, -1): (3, 2), (1, 0): (4, 3), (1, 3): (5, 4), (2, -1): (6, 5), (2, 8): (7, 6), (3, -1): (None, 7),
        (3, 2): (8, None), (3, 3): (None, 8), (3, 4): (9, None), (3, 7): (10, 9),
    }
    MAXIMA = {(1, -1): 0, (1, 5): 1, (2, 0): 2, (2, 3): 3, (3, -1): 4, (3, 0): 5, (3, 1): 6, (3, 7): 7}
    TURNS = {(1, -1): 4, (1, 1): 5, (1, 5): 6, (1, 7): 7, (3, 1): 8, (3, 3): 9, (3, 5): 10, (3, 7): 11}
    CODES = {(1, -1): 3, (1, 0): 4, (1, 3): 5, (2, -1): 6, (2, 8): 7, (3, 2): 8, (3, 4): 9, (3, 6): 10}
    HALF_NORMS = ((1, 6), (2, 13))
    EARLY = 3

    def ahead(b, t, more2):
        return [(b + 1 + t // T, t % T)] if t < T or more2 else []

    table = nc.dram_tensor("h0_table", (B * ROWS, C), F32).ap()
    table_v = table.rearrange("(b r) c -> b r c", r=ROWS)
    x_v = x.rearrange("b (t p) c -> b p t c", p=P)
    out_v = out.rearrange("b (t p) c -> b p t c", p=P)
    adj_v = adj.rearrange("b (t p) n -> b t p n", p=P)

    with ExitStack() as ctx:
        def sb(name, shape, dt=F32):
            return ctx.enter_context(nc.sbuf_tensor(name, shape, dt))

        def ps(name, shape, dt=F32):
            return ctx.enter_context(nc.psum_tensor(name, shape, dt))

        def sem(name):
            return ctx.enter_context(nc.semaphore(name))

        ident = sb("ident", [P, P])
        ident_bf = sb("ident_bf", [P, P], BF16)
        ones = sb("ones", [P, P])
        quad_bits = sb("quad_bits", [P, P // QUAD], BF16)
        code_base = sb("code_base", [P, Q])
        bit_of = sb("bit_of", [P, QUAD], I32)
        place = sb("place", [P, QUAD])
        first_row = sb("first_row", [P, 1])
        w0_sb = sb("w0_sb", [P, 2, C])
        b0_row = sb("b0_row", [1, C])
        wr = [None] + [sb(f"wr{l}", [P, C + 3 * HEADS[l]]) for l in (1, 2, 3)]
        wa1 = [None] + [sb(f"wa1_{l}", [P, HEADS[l], P]) for l in (1, 2, 3)]
        b2_all = sb("b2_all", [P, C + 3 * HM])
        b2_col = sb("b2_col", [P, 1])
        adj_in = sb("adj_in", [P, N], I32)
        adj_bf = sb("adj_bf", [P, N], BF16)
        mask_next = sb("mask_next", [P, T, N], BF16)
        mask = sb("mask", [P, T, N], BF16)
        edges = sb("edges", [P, HM, T, N], BF16)
        codes = sb("codes", [P, Q])
        top = sb("top", [P, KV])
        top_near = sb("top_near", [P, KV])
        top_int = sb("top_int", [P, KV], I32)
        quad_up = sb("quad_up", [P, KV], I32)
        bits = sb("bits", [P, KV, QUAD], I32)
        near = sb("near", [P, KV * QUAD])
        index = sb("index", [P, T, KV], U32)
        idle = sb("idle", [1, 2])
        gathered = sb("gathered", [P, SLOTS, S * C])
        agg = sb("agg", [P, T, C])
        x_next = sb("x_next", [P, T, C])
        xc = sb("xc", [P, T, C])
        h = sb("h", [P, T, C])
        hT = sb("hT", [P, N])
        stats = sb("stats", [P, T, 6])
        meanvar_one = sb("meanvar_one", [P, T, 2])
        meanvar = sb("meanvar", [P, B, T, 2])
        var = sb("var", [P, B, T])
        root = sb("root", [P, B, T])
        rstd = sb("rstd", [P, B, T])
        shift = sb("shift", [P, B, T])
        wh = sb("wh", [P, T, C + 3 * HM])
        top_s2 = sb("top_s2", [P, HM])
        top_row = sb("top_row", [HM, 1])
        top_diag = sb("top_diag", [HM, HM])
        top_all = sb("top_all", [P, HM])
        s2_rel = sb("s2_rel", [P, T * HM])
        t_all = sb("t_all", [P, T * HM])
        t_neg = sb("t_neg", [P, T * HM])
        t_pos = sb("t_pos", [P, T * HM])
        s2_steep = sb("s2_steep", [P, T * HM])
        f1 = sb("f1", [P, T * HM])
        f2 = sb("f2", [P, T * HM])
        f2n = sb("f2n", [P, T * HM])
        e1 = sb("e1", [P, T * HM])
        e2 = sb("e2", [P, T * HM])
        cols = sb("cols", [P, T * 2 * (C + HM)])
        part = sb("part", [P, 3, T * 2 * (C + HM)], BF16)
        npart = sb("npart", [P, 3, T * (C + HM)], BF16)
        rden = sb("rden", [P, 2, HM // 2])
        numer = cols[:, 0:2 * (C + 1)].rearrange("p (k c) -> p k c", k=2)
        y = cols[:, 2 * (C + 1):4 * C + 2].rearrange("p (k c) -> p k c", k=2)
        y_neg = cols[:, 4 * C + 2:6 * C + 2].rearrange("p (k c) -> p k c", k=2)
        halves = cols[:, 8 * C:8 * C + 8 * (C + 1)].rearrange("p (k s c) -> p k s c", k=4, s=2)
        aggT = wh[:, :, :].rearrange("p t c -> p (t c)")[:, 0:N]
        room = edges[:, :, :, :].bitcast(F32).rearrange("p h t n -> p (h t n)")
        x_all = room[:, 0:B * T * C].rearrange("p (b t c) -> p b t c", b=B, t=T)
        h_all = room[:, B * T * C:2 * B * T * C].rearrange("p (b t c) -> p b t c", b=B, t=T)
        b2_row = aggT[0:1, 2 * P:2 * P + C + 3 * HM]
        w_turned = (hT[:, C:2 * C], hT[:, 2 * C:3 * C])

        ps_mask = ps("ps_mask", [P, T, P], BF16)
        ps_x = ps("ps_x", [P, 2, 512])
        ps_s = ps("ps_s", [P, 2, 512])
        ps_acc = ps("ps_acc", [P, 2, 512])
        ps_small = ps("ps_small", [P, 512])
        ps_code = ps_small[:, 512 - Q:512]
        ps_w = [ps_acc[:, 0, :], ps_acc[:, 1, :]]
        ps_wa = [ps_s[:, 0, :], ps_acc[:, 0, :], ps_acc[:, 1, :]]

        def s1_row(g):
            return (ps_s, ps_x)[g % 2][:, :, :]

        weights_in = sem("weights_in")
        consts_ready = sem("consts_ready")
        diag_ready = sem("diag_ready")
        wprep_ps = sem("wprep_ps")
        wprep_sb = sem("wprep_sb")
        weights_ready = sem("weights_ready")
        all_loaded = [sem("first_loaded"), sem("others_loaded")]
        x_loaded = sem("x_loaded")
        h0_loaded = sem("h0_loaded")
        table_stored = [sem("first_stored"), sem("others_stored")]
        rows_stored = [sem("rows_stored0"), sem("rows_stored1")]
        adj_loaded = sem("adj_loaded")
        gather_done = [sem(f"gather_done{k}") for k in range(SLOTS)]
        chain_done = sem("chain_done")
        adj_cast = sem("adj_cast")
        mask_ps = sem("mask_ps")
        mask_next_ready = sem("mask_next_ready")
        mask_ready = sem("mask_ready")
        codes_ps = sem("codes_ps")
        codes_used = sem("codes_used")
        index_ready = sem("index_ready")
        idle_done = sem("idle_done")
        gather_free = sem("gather_free")
        norm_ready = sem("norm_ready")
        h_ready = sem("h_ready")
        turned_ps = sem("turned_ps")
        turned_sb = sem("turned_sb")
        sage_ps = sem("sage_ps")
        sage_used = sem("sage_used")
        wh_ps = sem("wh_ps")
        wh_sb = sem("wh_sb")
        s1_ps = sem("s1_ps")
        top_ready = sem("top_ready")
        top_turned = sem("top_turned")
        top_diag_ready = sem("top_diag_ready")
        top_spread = sem("top_spread")
        exp_in_ready = sem("exp_in_ready")
        exp_ready = sem("exp_ready")
        steep_ready = sem("steep_ready")
        cols_ready = sem("cols_ready")
        hi_ready = sem("hi_ready")
        rest_ready = sem("rest_ready")
        mid_ready = sem("mid_ready")
        lo_ready = sem("lo_ready")
        nparts_ready = sem("nparts_ready")
        rough_ready = sem("rough_ready")
        edges_ready = sem("edges_ready")
        acc_ready = sem("acc_ready")
        acc_used = sem("acc_used")
        pairs_used = sem("pairs_used")
        y_neg_ready = sem("y_neg_ready")
        elu_ready = sem("elu_ready")
        x_done = sem("x_done")

        block = ctx.enter_context(nc.Block())

        @block.sync
        def _(sp):
            def load(dst, src):
                sp.dma_start(dst, src, allow_slow_non_contiguous=True).then_inc(weights_in, 16)

            def load_adj(b, t):
                if not (isinstance(b, int) and b * T + t == 0):
                    sp.wait_ge(adj_cast, b * T + t)
                sp.dma_start(adj_in[:, :], adj_v[b, t]).then_inc(adj_loaded, 16)

            def table_rows(b):
                return table_v[b, 0:N, :].rearrange("(t p) c -> p t c", p=P)

            def store_half(b, half):
                ts = slice(half * T // 2, (half + 1) * T // 2)
                sp.wait_ge(x_done, 2 * b + half + 1)
                sp.dma_start(out_v[b][:, ts, :], xc[:, ts, :]).then_inc(rows_stored[half], 16)

            def turn(b, more, more2):
                if more:
                    for t in range(EARLY + 3, T + EARLY + 3):
                        if t == T + EARLY - 1:
                            sp.wait_ge(turned_ps, 10 * (b + 1))
                            sp.dma_start(h[:, :, :], table_rows(b + 1)).then_inc(h0_loaded, 16)
                        for at in ahead(b, t, more2):
                            load_adj(*at)
                        if t == T + EARLY + 1:
                            store_half(b, 0)
                        if t == EARLY + 3:
                            sp.wait_ge(sage_used, 2 * b + 2)
                            sp.dma_start(x_next[:, :, :], x_v[b + 1]).then_inc(x_loaded, 16)
                else:
                    store_half(b, 0)
                store_half(b, 1)

            def store_table(b):
                sp.wait_ge(h_ready, T * (b + 1))
                sp.dma_start(table_rows(b), h_all[:, b]).then_inc(table_stored[min(b, 1)], 16)

            for b in range(B):
                sp.dma_start(x_all[:, b], x_v[b]).then_inc(all_loaded[min(b, 1)], 16)
                if b == 0:
                    load_adj(0, 0)
            sp.wait_ge(consts_ready, 3)
            for half in range(2):
                bs = slice(half * B // 2, (half + 1) * B // 2)
                sp.dma_start(table_v[bs, N, :], aggT[bs, N - C:N]).then_inc(rows_stored[half], 16)
            load_adj(0, 1)
            load_adj(0, 2)
            store_table(0)
            load_adj(0, 3)
            load(w0_sb[:, :, :], w0.rearrange("(s k) o -> k s o", k=P))
            load(b0_row[:, :], b0.rearrange("(a n) -> a n", a=1))
            load(b2_row[:, 0:C], b2.rearrange("(a n) -> a n", a=1))
            load(b2_col[:, :], b2.rearrange("(n a) -> n a", a=1))
            load(wr[1][:, 0:C], w1)
            load(wr[3][:, 0:C], w3)
            load(hT[:, 0:C], w2)
            for l, a in ((1, a1), (3, a3)):
                for s in range(2):
                    load(aggT[:, 2 * l + s:2 * l + s + 1], a[s * C:(s + 1) * C, :])
            D = C // HM
            for s in range(2):
                for g in range(HM):
                    load(aggT[g * D:(g + 1) * D, 16 + s * HM + g:17 + s * HM + g],
                         a2[g, s * D:(s + 1) * D].rearrange("(d a) -> d a", a=1))
            for b in range(1, B):
                store_table(b)
            sp.dma_start(x_next[:, :, :], x_v[0]).then_inc(x_loaded, 16)
            sp.wait_ge(table_stored[0], 16)
            sp.dma_start(h[:, :, :], table_rows(0)).then_inc(h0_loaded, 16)
            for t in range(4, T):
                load_adj(0, t)
            for t in range(EARLY + 3):
                load_adj(1, t)
            with sp.Fori(0, B - 2) as b:
                turn(b, True, True)
            turn(B - 2, True, False)
            turn(B - 1, False, False)
            for half in range(2):
                sp.wait_ge(rows_stored[half], 16 + 16 * B)

        @block.gpsimd
        def _(pool):
            nc.gpsimd.iota(code_base[:, :], pattern=[[-16, Q]], base=16 * Q, channel_multiplier=0,
                           allow_small_or_imprecise_dtypes=True).then_inc(diag_ready, 1)
            nc.gpsimd.memset(idle[:, :], 0.0).then_inc(diag_ready, 1)
            pool.wait_ge(diag_ready, 2)
            pool.wait_ge(consts_ready, 2)
            for m in (ident_bf, ident):
                nc.gpsimd.affine_select(out=m[:, :], in_=m[:, :], compare_op=ALU.not_equal, fill=1.0, base=0,
                                        pattern=[[-1, P]], channel_multiplier=1).then_inc(diag_ready, 1)
            nc.gpsimd.memset(quad_bits[:, :], 0.0).then_inc(diag_ready, 1)
            for k in range(QUAD):
                pool.wait_ge(diag_ready, 5 + k)
                nc.gpsimd.affine_select(out=quad_bits[:, :], in_=quad_bits[:, :], compare_op=ALU.not_equal,
                                        fill=float(8 >> k), base=-k, pattern=[[-QUAD, P // QUAD]],
                                        channel_multiplier=1).then_inc(diag_ready, 1)
            def gather(b, t, rows):
                pool.wait_ge(index_ready, b * T + t + 1)
                nc.gpsimd.tensor_tensor(idle[:, 1:2], idle[:, 0:1], idle[:, 0:1], ALU.add)\
                  .then_inc(idle_done, 1)
                pool.wait_ge(gather_free, 1)
                pool.wait_ge(gather_free, b * T + t + (t < 2))
                pool.wait_ge(idle_done, b * T + t + 1)
                for k in range(S):
                    nc.gpsimd.indirect_dma_start(
                        out=gathered[:, t % SLOTS, k * C:(k + 1) * C], out_offset=None, in_=rows,
                        in_offset=bass.IndirectOffsetOnAxis(ap=index[:, t, k:k + 1], axis=0),
                    ).then_inc(gather_done[t % SLOTS], 16)

            for half in range(2):
                pool.wait_ge(rows_stored[half], 16)
            pool.wait_ge(table_stored[0], 16)
            for t in range(T):
                gather(0, t, table[0:ROWS, :])
            pool.wait_ge(table_stored[1], 16 * (B - 1))
            with pool.Fori(1, B) as b:
                for t in range(T):
                    gather(b, t, table)

        @block.vector
        def _(dve):
            step = Chain(dve, chain_done)

            def row_stats(src, t):
                step(nc.vector.bn_stats(out=stats[:, t, :], in_=src[:, t, :]))

            def invert(bs, ts=slice(0, T)):
                v, r, q = var[:, bs, ts], rstd[:, bs, ts], root[:, bs, ts]
                step(nc.vector.tensor_scalar(v, meanvar[:, bs, ts, 1], EPS, None, ALU.add))
                step.settle()
                step(nc.vector.tensor_scalar(q.bitcast(I32), v.bitcast(I32), 1, None, ALU.logical_shift_right))
                step.settle()
                step(nc.vector.tensor_scalar(r.bitcast(I32), q.bitcast(I32), -1.0, float(RSQRT_SEED),
                                             ALU.mult, ALU.add))
                step.settle()
                for _ in range(3):
                    step(nc.vector.tensor_tensor(q, r, r, ALU.mult))
                    step.settle()
                    step(nc.vector.scalar_tensor_tensor(out=q, in0=q, scalar=-0.5, in1=v,
                                                        op0=ALU.mult, op1=ALU.mult))
                    step.settle()
                    step(nc.vector.scalar_tensor_tensor(out=r, in0=q, scalar=1.5, in1=r,
                                                        op0=ALU.add, op1=ALU.mult))
                    step.settle()
                nc.vector.scalar_tensor_tensor(out=shift[:, bs, ts], in0=meanvar[:, bs, ts, 0], scalar=-1.0, in1=r,
                                               op0=ALU.mult, op1=ALU.mult).then_inc(norm_ready, 1)

            def norm(tiles):
                step.settle()
                for t in tiles:
                    step(nc.vector.bn_aggr(out=meanvar[:, 0, t, :], in_=stats[:, t, :]))
                step.settle()
                invert(slice(0, 1), slice(tiles[0], tiles[-1] + 1))

            def largest(*pairs):
                done = [step.n for _ in pairs]
                for r in range(KV // 8):
                    for i, (src, dst) in enumerate(pairs):
                        step.settle(done[i])
                        step(nc.vector.max(out=dst[:, 8 * r:8 * r + 8], in_=src[:, :]))
                        done[i] = step.n
                    if r < KV // 8 - 1:
                        for i, (src, dst) in enumerate(pairs):
                            step.settle(done[i])
                            step(nc.vector.match_replace(out=src[:, :], in_to_replace=dst[:, 8 * r:8 * r + 8],
                                                         in_values=src[:, :], imm_value=0.0))
                            done[i] = step.n
                step.settle()

            def list_parts(quads_of, neighbours_of):
                pairs = []
                step.settle()
                if neighbours_of:
                    b, t = neighbours_of
                    dve.wait_ge(codes_used, b * T + t + 1)
                    step(nc.vector.tensor_scalar(quad_up[:, :], top_int[:, :], 4, None, ALU.logical_shift_right))
                    up_done = step.n
                    step(nc.vector.tensor_tensor(
                        bits[:, :, :], top_int[:, :].unsqueeze(2).to_broadcast([P, KV, QUAD]),
                        bit_of[:, :].unsqueeze(1).to_broadcast([P, KV, QUAD]), ALU.bitwise_and))
                    near_v = near[:, :].rearrange("p (k q) -> p k q", q=QUAD)
                    step.settle(up_done)
                    step(nc.vector.scalar_tensor_tensor(
                        out=near_v, in0=quad_up[:, :].unsqueeze(2).to_broadcast([P, KV, QUAD]), scalar=float(QUAD),
                        in1=place[:, :].unsqueeze(1).to_broadcast([P, KV, QUAD]), op0=ALU.mult, op1=ALU.subtract))
                    near_done = step.n
                if quads_of:
                    b, t = quads_of
                    dve.wait_ge(codes_ps, b * T + t + 1)
                    step(nc.vector.scalar_tensor_tensor(out=codes[:, :], in0=ps_code, scalar=0.0,
                                                        in1=code_base[:, :], op0=ALU.is_gt, op1=ALU.mult))
                    pairs.append((codes, top))
                if neighbours_of:
                    step.settle(near_done)
                    step(nc.vector.scalar_tensor_tensor(out=near_v, in0=bits[:, :, :], scalar=0.0, in1=near_v,
                                                        op0=ALU.is_gt, op1=ALU.mult))
                    pairs.append((near, top_near))
                if quads_of:
                    step.settle(step.n - (1 if neighbours_of else 0))
                    step(nc.vector.tensor_tensor(codes[:, :], codes[:, :], ps_code, ALU.add))
                largest(*pairs)
                if quads_of:
                    nc.vector.tensor_copy(top_int[:, :], top[:, :]).then_inc(codes_used, 1)
                if neighbours_of:
                    t = neighbours_of[1]
                    nc.vector.tensor_scalar(index[:, t, :], top_near[:, :], -1.0, first_row[:, 0:1],
                                            ALU.mult, ALU.add).then_inc(index_ready, 1)

            def next_rows():
                step.settle()
                step(nc.vector.tensor_scalar(first_row[:, :], first_row[:, :], float(ROWS), None, ALU.add))
                step.settle()

            def take_maximum(b, t):
                of_slot = len(range(t % SLOTS, T, SLOTS))
                dve.wait_ge(gather_done[t % SLOTS], b * (16 * S * of_slot) + 16 * S * (t // SLOTS + 1))
                nc.vector.tensor_reduce(agg[:, t, :], gathered[:, t % SLOTS, :].rearrange("p (k c) -> p c k", k=S),
                                        AX.X, ALU.max).then_inc(gather_free, 1)

            def beside(b, layer, i, more2):
                if (layer, i) in MAXIMA:
                    take_maximum(b + 1, MAXIMA[layer, i])
                if (layer, i) in LISTS:
                    quads_of, neighbours_of = ([] if t is None else ahead(b, t, more2) for t in LISTS[layer, i])
                    if LISTS[layer, i][1] == T and neighbours_of:
                        next_rows()
                    if quads_of or neighbours_of:
                        list_parts(*(at[0] if at else None for at in (quads_of, neighbours_of)))

            def attention(b, layer, more, more2):
                H, D1 = HEADS[layer], width(layer)
                D = D1 - 1
                HT = T * H
                m = b * 3 + (layer - 1)
                s1 = wh[:, :, C:C + H]
                s2 = wh[:, :, C + H:C + 2 * H]
                minus_s2 = wh[:, :, C + 2 * H:C + 3 * H]

                def small(tile):
                    return tile[:, 0:HT].rearrange("p (t h) -> p t h", h=H)

                def mark_edges(g, tiles):
                    k = G0[layer] + g
                    for t in tiles:
                        dve.wait_ge(rough_ready, b * NR + rough_count(k, t if shared(k, t) else ALONE - 1))
                        if shared(k, t):
                            ins = nc.vector.tensor_tensor(edges[:, g, t, :], edges[:, g, t, :], mask[:, t, :], ALU.min)
                        else:
                            ins = nc.vector.scalar_tensor_tensor(
                                out=edges[:, g, t, :], in0=s1_row(k).rearrange("p a n -> p (a n)"),
                                scalar=minus_s2[:, t, g:g + 1], in1=mask[:, t, :],
                                op0=ALU.is_gt, op1=ALU.mult)
                        ins.then_inc(edges_ready, 1)

                dve.wait_ge(wh_sb, b * 24 + 8 * layer)
                if layer == 2:
                    step(nc.vector.tensor_tensor(wh[:, :, :], wh[:, :, :],
                                                 b2_all[:, :].unsqueeze(1).to_broadcast([P, T, C + 3 * H]), ALU.add))
                    step.settle()
                nc.vector.tensor_reduce(top_s2[:, 0:H], s2.rearrange("p t h -> p h t"), AX.X, ALU.max)\
                  .then_inc(top_ready, 1)
                nc.vector.tensor_scalar(small(s2_steep), minus_s2, -STEEP, None, ALU.mult).then_inc(steep_ready, 1)
                dve.wait_ge(top_turned, m + 1)
                step(nc.vector.tensor_reduce(top_row[0:H, :], ps_small[0:H, 0:P], AX.X, ALU.max))
                step.settle()
                nc.vector.tensor_scalar(top_diag[0:H, 0:H], ident[0:H, 0:H], top_row[0:H, 0:1], None, ALU.mult)\
                  .then_inc(top_diag_ready, 1)
                dve.wait_ge(top_spread, m + 1)
                step(nc.vector.tensor_copy(top_all[:, 0:H], ps_small[:, 0:H]))
                step.settle()
                spread = top_all[:, 0:H].unsqueeze(1).to_broadcast([P, T, H])
                step(nc.vector.tensor_tensor(small(s2_rel), s2, spread, ALU.subtract))
                step(nc.vector.tensor_tensor(small(t_all), s1, spread, ALU.add))
                step.settle()
                nc.vector.tensor_scalar(t_neg[:, 0:HT], t_all[:, 0:HT], 0.0, None, ALU.min).then_inc(exp_in_ready, 1)
                nc.vector.tensor_scalar(t_pos[:, 0:HT], t_all[:, 0:HT], 0.0, None, ALU.max).then_inc(exp_in_ready, 1)
                dve.wait_ge(exp_ready, 2 * m + 1)
                step(nc.vector.tensor_scalar(f2n[:, 0:HT], f2[:, 0:HT], -1.0, None, ALU.mult))
                step.settle()
                cv = cols[:, 0:HT * 2 * D1].rearrange("p (t h s d) -> p t h s d", h=H, s=2, d=D1)
                whv = wh[:, :, 0:C].rearrange("p t (h d) -> p t h d", d=D)
                W = TC * H * 2 * D1
                for c in range(CH):
                    ts = slice(c * TC, (c + 1) * TC)
                    for s, f in enumerate((f1, f2n)):
                        step(nc.vector.tensor_tensor(cv[:, ts, :, s, 0:D], whv[:, ts],
                                                     small(f)[:, ts].unsqueeze(3).to_broadcast([P, TC, H, D]),
                                                     ALU.mult))
                        ins = nc.vector.tensor_copy(cv[:, ts, :, s, D], small(f)[:, ts])
                        if s:
                            ins.then_inc(cols_ready, 1)
                        else:
                            step(ins)
                step.settle()
                for c in range(CH):
                    dve.wait_ge(hi_ready, b * (3 * CH) + CH * (layer - 1) + c + 1)
                    nc.vector.tensor_tensor(cols[:, c * W:(c + 1) * W], cols[:, c * W:(c + 1) * W],
                                            part[:, 0, c * W:(c + 1) * W], ALU.subtract).then_inc(rest_ready, 1)
                if layer == 2:
                    mark_edges(0, range(0, 1))
                for c in range(CH):
                    dve.wait_ge(mid_ready, b * (3 * CH) + CH * (layer - 1) + c + 1)
                    dve.wait_ge(rest_ready, b * (3 * CH) + CH * (layer - 1) + c + 1)
                    step(nc.vector.tensor_tensor(part[:, 2, c * W:(c + 1) * W], cols[:, c * W:(c + 1) * W],
                                                 part[:, 1, c * W:(c + 1) * W], ALU.subtract))
                    step.settle()
                    nc.vector.tensor_scalar(
                        npart[:, :, c * W // 2:(c + 1) * W // 2].rearrange("p k (q d) -> p k q d", d=D1),
                        part[:, :, c * W:(c + 1) * W].rearrange("p k (q s d) -> p k q s d", s=2, d=D1)[:, :, :, 1, :],
                        -1.0, None, ALU.mult).then_inc(nparts_ready, 1)
                mark_edges(0, range(int(layer == 2), T))
                HG = H // GROUPS[layer]
                for g in range(1, HG):
                    mark_edges(g, range(T))

                for i in range(GROUPS[layer] * T):
                    t, g0 = i % T, i // T * HG
                    if (layer, i) in HALF_NORMS:
                        norm(range(T // 2))
                    if more:
                        beside(b, layer, i, more2)
                    for g, j in second_group(layer, i - 1):
                        mark_edges(g, [j])
                    if i % 2 == 0:
                        continue
                    n = b * NA + A0[layer] + i
                    dve.wait_ge(acc_used, n + 1)
                    step.settle()
                    if layer == 3 and i == T // 2 + 1:
                        dve.wait_ge(x_done, 2 * b + 1)
                    pair = halves[:, i % 4 - 1:i % 4 + 1, :, 0:HG * D1]
                    nc.vector.tensor_tensor(numer[:, :, 0:HG * D1], pair[:, :, 0, :], pair[:, :, 1, :], ALU.add)\
                      .then_inc(pairs_used, 1)
                    dve.wait_ge(pairs_used, b * (NA // 2) + (A0[layer] + i + 1) // 2)
                    nv = numer[:, :, 0:HG * D1].rearrange("p k (h d) -> p k h d", d=D1)
                    step(nc.vector.reciprocal(rden[:, :, 0:HG], nv[:, :, :, D]))
                    step.settle()
                    if layer == 1:
                        if i > 1:
                            add_elu(b, i // 2 - 1)
                        step(nc.vector.tensor_tensor(y[:, :, :], numer[:, :, 0:D],
                                                     rden[:, :, 0:1].to_broadcast([P, 2, D]), ALU.mult))
                        step.settle()
                        nc.vector.tensor_scalar(y_neg[:, :, :], y[:, :, :], 0.0, None, ALU.min)\
                          .then_inc(y_neg_ready, 1)
                        xs = xc[:, t - 1:t + 1, :]
                        step(nc.vector.scalar_tensor_tensor(out=xs, in0=y[:, :, :], scalar=0.0, in1=xs,
                                                            op0=ALU.max, op1=ALU.add))
                    else:
                        for k in range(2):
                            for g in range(HG):
                                xs = xc[:, t - 1 + k, (g0 + g) * D:(g0 + g + 1) * D]
                                ins = nc.vector.scalar_tensor_tensor(
                                    out=xs, in0=numer[:, k, g * D1:g * D1 + D], scalar=rden[:, k, g:g + 1], in1=xs,
                                    op0=ALU.mult, op1=ALU.add)
                                if layer == 3 and k and i % (T // 2) == T // 2 - 1:
                                    ins.then_inc(x_done, 1)
                                else:
                                    step(ins)
                        if layer == 2 and g0 + HG == H:
                            step.settle()
                            for k in range(2):
                                row_stats(xc, t - 1 + k)
                if layer == 1:
                    add_elu(b, T // 2 - 1)

            def add_elu(b, pair):
                dve.wait_ge(elu_ready, b * (T // 2) + pair + 1)
                step.settle()
                xs = xc[:, 2 * pair:2 * pair + 2, :]
                step(nc.vector.scalar_tensor_tensor(out=xs, in0=y_neg[:, :, :], scalar=-1.0, in1=xs,
                                                    op0=ALU.add, op1=ALU.add))
                step.settle()
                for k in range(2):
                    row_stats(xc, 2 * pair + k)

            def turn(b, more, more2):
                dve.wait_ge(x_loaded, b * 16 + 16)
                for half in range(2):
                    tiles = range(half * 4, half * 4 + 4)
                    ts = slice(half * 4, half * 4 + 4)
                    dve.wait_ge(sage_ps, 2 * b + half + 1)
                    dve.wait_ge(rows_stored[half], b * 16 + 16)
                    nc.vector.scalar_tensor_tensor(
                        out=xc[:, ts, :], in0=ps_s[:, half, :].rearrange("p (t c) -> p t c", c=C), scalar=0.0,
                        in1=x_next[:, ts, :], op0=ALU.max, op1=ALU.add).then_inc(sage_used, 1)
                    dve.wait_ge(sage_used, 2 * b + half + 1)
                    for t in tiles:
                        row_stats(xc, t)
                    norm(tiles)
                for layer in (1, 2, 3):
                    if layer > 1:
                        norm(range(T // 2, T))
                    if more:
                        beside(b, layer, -1, more2)
                    attention(b, layer, more, more2)

            nc.vector.memset(ident[:, :], 0.0).then_inc(consts_ready, 1)
            nc.vector.memset(ident_bf[:, :], 0.0).then_inc(consts_ready, 1)
            nc.vector.memset(aggT[:, 16:N], 0.0).then_inc(consts_ready, 1)
            nc.vector.memset(first_row[:, :], float(N)).then_inc(gather_free, 2)
            step(nc.vector.memset(ones[:, :], 1.0))
            for k in range(QUAD):
                step(nc.vector.memset(bit_of[:, k:k + 1], 8 >> k))
                step(nc.vector.memset(place[:, k:k + 1], float(k)))

            def table_stats(b):
                for t in range(T):
                    step(nc.vector.bn_stats(out=stats[:, t, :], in_=x_all[:, b, t, :]))
                step.settle()
                for t in range(T):
                    step(nc.vector.bn_aggr(out=meanvar_one[:, t, :], in_=stats[:, t, :]))
                step.settle()
                step(nc.vector.tensor_copy(meanvar[:, b, :, :], meanvar_one[:, :, :]))
                step.settle()

            dve.wait_ge(all_loaded[0], 16)
            table_stats(0)
            invert(slice(0, 1))
            dve.wait_ge(diag_ready, 1)
            dve.wait_ge(gather_free, 2)
            list_parts((0, 0), None)
            for t in range(1, SLOTS):
                list_parts((0, t), (0, t - 1))
            dve.wait_ge(all_loaded[1], 16 * (B - 1))
            step.restart()
            with dve.Fori(1, B) as b:
                table_stats(b)
                step.restart()
            invert(slice(1, B))
            for n, l in enumerate((1, 3, 2)):
                H = HEADS[l]
                if l == 2:
                    dve.wait_ge(wprep_ps, 5)
                    step(nc.vector.tensor_copy(wr[2][:, 0:C], ps_x[:, 0, 0:C]))
                    step(nc.vector.tensor_copy(b2_row[:, C:C + 2 * H], ps_wa[2][0:1, 64:64 + 2 * H]))
                    step.settle()
                    nc.vector.scalar_tensor_tensor(
                        out=b2_row[:, C + 2 * H:C + 3 * H], in0=b2_row[:, C:C + H], scalar=-1.0,
                        in1=b2_row[:, C + H:C + 2 * H], op0=ALU.mult, op1=ALU.subtract).then_inc(wprep_sb, 1)
                    dve.wait_ge(wprep_ps, 6)
                    step(nc.vector.tensor_copy(b2_all[:, :], ps_x[:, 1, 0:C + 3 * H]))
                else:
                    dve.wait_ge(wprep_ps, 2 * n + 1)
                    nc.vector.tensor_copy(w_turned[n], ps_x[:, n, 0:C]).then_inc(wprep_sb, 1)
                    dve.wait_ge(wprep_ps, 2 * n + 2)
                step(nc.vector.tensor_copy(wr[l][:, C:C + 2 * H], ps_wa[n][:, 0:2 * H]))
                step(nc.vector.tensor_scalar(wr[l][:, C + 2 * H:C + 3 * H], ps_wa[n][:, H:2 * H],
                                             -1.0, None, ALU.mult))
                step.settle()
                for g in range(H):
                    nc.vector.tensor_scalar(wa1[l][:, g, :], ones[:, :], wr[l][:, C + g:C + g + 1], None,
                                            ALU.mult).then_inc(weights_ready, 1)
            for t in range(SLOTS, T):
                list_parts((0, t), (0, t - 1))
                take_maximum(0, t - SLOTS)
            list_parts((1, 0), (0, T - 1))
            take_maximum(0, T - SLOTS)
            next_rows()
            for t in range(1, EARLY):
                list_parts((1, t), (1, t - 1))
                take_maximum(0, T - SLOTS + t)
            step.restart()
            with dve.Fori(0, B - 2) as b:
                turn(b, True, True)
                step.restart()
            turn(B - 2, True, False)
            turn(B - 1, False, False)

        @block.scalar
        def _(act):
            def norm(src, dst, k, tiles):
                for t in tiles:
                    nc.scalar.activation(dst[:, t, :], src[:, t, :], ACT.Relu, bias=shift[:, k, t:t + 1],
                                         scale=rstd[:, k, t:t + 1]).then_inc(h_ready, 1)

            def cast_mask(b, t):
                n = b * T + t
                act.wait_ge(adj_loaded, b * (16 * T) + 16 * (t + 1))
                if not (isinstance(b, int) and n == 0):
                    act.wait_ge(mask_ps, n)
                nc.scalar.activation(adj_bf[:, :], adj_in[:, :], ACT.Copy).then_inc(adj_cast, 1)

            def keep_mask(b, t):
                act.wait_ge(mask_ps, b * T + t + 1)
                if not (isinstance(b, int) and b == 0):
                    act.wait_ge(mask_ready, (b - 1) * T + t + 1)
                nc.scalar.activation(mask_next[:, :, t * P:(t + 1) * P], ps_mask[:, :, :], ACT.Copy)\
                  .then_inc(mask_next_ready, 1)

            def keep_and_cast(b, t, more2):
                for at in ahead(b, t, more2):
                    keep_mask(*at)
                for at in ahead(b, t + 1, more2):
                    cast_mask(*at)

            def bring_forward(b, t):
                nc.scalar.activation(mask[:, :, t * P:(t + 1) * P], mask_next[:, :, t * P:(t + 1) * P], ACT.Copy)\
                  .then_inc(mask_ready, 1)

            def keep_turned(b, s, half, dst):
                act.wait_ge(turned_ps, b * 10 + 2 * s + half + 1)
                nc.scalar.activation(dst[:, half * 512:(half + 1) * 512], ps_x[:, half, :], ACT.Copy)\
                  .then_inc(turned_sb, 1)

            def rough_edges(b, k, tiles):
                layer = max(l for l in (1, 2, 3) if k >= G0[l])
                g = k - G0[layer]
                act.wait_ge(s1_ps, b * NG + k + 1)
                for t in tiles:
                    at = t * HEADS[layer] + g
                    nc.scalar.activation(edges[:, g, t, :], s1_row(k).rearrange("p a n -> p (a n)"), ACT.Relu,
                                         bias=s2_steep[:, at:at + 1], scale=STEEP).then_inc(rough_ready, 1)

            def attention(b, layer):
                H, D1 = HEADS[layer], width(layer)
                HT = T * H
                W = TC * H * 2 * D1
                if layer == 1:
                    act.wait_ge(norm_ready, b * 6 + 3)
                    norm(xc, h, 0, range(T // 2))
                keep_turned(b, layer + 1, 0, hT)
                act.wait_ge(norm_ready, b * 6 + 2 * layer + 2)
                norm(xc, h, 0, range(T // 2, T))
                keep_turned(b, layer + 1, 1, hT)
                for t in range(T):
                    act.wait_ge(wh_ps, b * 24 + 8 * (layer - 1) + t + 1)
                    nc.scalar.activation(wh[:, t, 0:C + 3 * H], ps_w[t % 2][:, 0:C + 3 * H], ACT.Copy)\
                      .then_inc(wh_sb, 1)
                act.wait_ge(steep_ready, b * 3 + layer)
                act.wait_ge(exp_in_ready, b * 6 + 2 * layer)
                nc.scalar.activation(f1[:, 0:HT], s2_rel[:, 0:HT], ACT.Exp)
                nc.scalar.activation(f2[:, 0:HT], s2_rel[:, 0:HT], ACT.Exp, scale=SLOPE)\
                  .then_inc(exp_ready, 1)
                for c in range(CH):
                    act.wait_ge(cols_ready, b * (3 * CH) + CH * (layer - 1) + c + 1)
                    nc.scalar.activation(part[:, 0, c * W:(c + 1) * W], cols[:, c * W:(c + 1) * W], ACT.Copy)\
                      .then_inc(hi_ready, 1)
                nc.scalar.activation(e1[:, 0:HT], t_neg[:, 0:HT], ACT.Exp, scale=1.0 - SLOPE)
                nc.scalar.activation(e2[:, 0:HT], t_pos[:, 0:HT], ACT.Exp, scale=SLOPE - 1.0)\
                  .then_inc(exp_ready, 1)
                for c in range(CH):
                    act.wait_ge(rest_ready, b * (3 * CH) + CH * (layer - 1) + c + 1)
                    nc.scalar.activation(part[:, 1, c * W:(c + 1) * W], cols[:, c * W:(c + 1) * W], ACT.Copy)\
                      .then_inc(mid_ready, 1)
                rough_edges(b, G0[layer], range(T if layer != 2 else ALONE))
                if layer == 2:
                    rough_edges(b, G0[2] + 1, range(T))
                for g, j in second_group(layer, -1):
                    rough_edges(b, G0[2] + g, [j])

            def scale_halves(b, layer, i):
                H, D1 = HEADS[layer], width(layer)
                HG = H // GROUPS[layer]
                t, g0 = i % T, i // T * HG
                act.wait_ge(acc_ready, b * NA + A0[layer] + i + 1)
                if i >= 4 and i % 2 == 0:
                    act.wait_ge(pairs_used, b * (NA // 2) + (A0[layer] + i) // 2 - 1)
                acc = ps_acc[:, i % 2, 0:2 * HG * D1].rearrange("p (h s d) -> p h s d", h=HG, s=2)
                for g in range(HG):
                    at = t * H + g0 + g
                    for s, e in enumerate((e1, e2)):
                        ins = nc.scalar.activation(halves[:, i % 4, s, g * D1:(g + 1) * D1], acc[:, g, s, :],
                                                   ACT.Copy, scale=e[:, at:at + 1])
                ins.then_inc(acc_used, 1)

            def elu_exp(b, pair):
                act.wait_ge(y_neg_ready, b * (T // 2) + pair + 1)
                nc.scalar.activation(y_neg[:, :, :], y_neg[:, :, :], ACT.Exp).then_inc(elu_ready, 1)

            def turn(b, more, more2):
                keep_turned(b, 1, 1, aggT)
                for layer in (1, 2, 3):
                    for i in range(-1, GROUPS[layer] * T):
                        if more and (layer, i) in TURNS:
                            keep_and_cast(b, TURNS[layer, i], more2)
                        if i < 0:
                            attention(b, layer)
                            continue
                        for g, j in second_group(layer, i):
                            rough_edges(b, G0[2] + g, [j])
                        scale_halves(b, layer, i)
                        if layer == 1 and i > 1 and i % 2:
                            elu_exp(b, i // 2 - 1)
                        if (layer, i - 1) in HALF_NORMS:
                            act.wait_ge(norm_ready, b * 6 + 2 * layer + 3)
                            norm(xc, h, 0, range(T // 2))
                        if more and layer == 3:
                            if i == 0:
                                act.wait_ge(mask_next_ready, b * T + 2 * T)
                            bring_forward(b + 1, i)
                            if i in H0_TURNS:
                                keep_turned(b + 1, 0, H0_TURNS.index(i), hT)
                    if layer == 1:
                        elu_exp(b, T // 2 - 1)
                if more:
                    keep_turned(b + 1, 1, 0, aggT)

            cast_mask(0, 0)
            for t in range(2):
                keep_mask(0, t)
                cast_mask(0, t + 1)
            act.wait_ge(norm_ready, 1)
            norm(x_all[:, 0], h_all[:, 0], 0, range(T))
            keep_mask(0, 2)
            cast_mask(0, 3)
            keep_mask(0, 3)
            act.wait_ge(norm_ready, 2)
            with act.Fori(1, B) as b:
                norm(x_all[:, b], h_all[:, b], b, range(T))
            for t in range(3, T):
                cast_mask((t + 1) // T, (t + 1) % T)
                if t < T - 1:
                    keep_mask(0, t + 1)
            act.wait_ge(mask_next_ready, T)
            for t in range(T):
                bring_forward(0, t)
            for half in range(2):
                keep_turned(0, 0, half, hT)
            keep_mask(1, 0)
            cast_mask(1, 1)
            keep_turned(0, 1, 0, aggT)
            for t in range(1, EARLY + 1):
                keep_mask(1, t)
                cast_mask(1, t + 1)
            with act.Fori(0, B - 2) as b:
                turn(b, True, True)
            turn(B - 2, True, False)
            turn(B - 1, False, False)

        @block.tensor
        def _(pe):
            def turn_mask(b, t):
                n = b * T + t
                pe.wait_ge(adj_cast, n + 1)
                if not (isinstance(b, int) and n == 0):
                    pe.wait_ge(mask_next_ready, n)
                for j in range(T):
                    ins = nc.tensor.transpose(ps_mask[:, j, :], adj_bf[:, j * P:(j + 1) * P], ident_bf[:, :])
                ins.then_inc(mask_ps, 1)

            def make_codes(b, t):
                n = b * T + t
                pe.wait_ge(mask_next_ready, n + 1)
                if not (isinstance(b, int) and n == 0):
                    pe.wait_ge(codes_used, n)
                for j in range(T):
                    ins = nc.tensor.matmul(ps_code[:, j * (P // QUAD):(j + 1) * (P // QUAD)],
                                           mask_next[:, j, t * P:(t + 1) * P], quad_bits[:, :],
                                           start=True, stop=True)
                ins.then_inc(codes_ps, 1)

            def turn_features(b, s, half, src, norms=None):
                if s:
                    pe.wait_ge(turned_sb, b * 10 + 2 * s + half - 1)
                for t in range(4 * half, 4 * half + 4):
                    if norms is not None:
                        pe.wait_ge(h_ready, norms + t + 1)
                    ins = nc.tensor.transpose(ps_x[:, half, t % 4 * P:(t % 4 + 1) * P], src[:, t, :], ident[:, :])
                ins.then_inc(turned_ps, 1)

            def turn_early(b, k):
                if k == 0:
                    pe.wait_ge(h0_loaded, b * 16 + 16)
                if k == 2:
                    pe.wait_ge(gather_free, b * T + T // 2 + 2)
                turn_features(b, k // 2, k % 2, (h, h, agg)[k])

            def sage_part(s, t, src, stop):
                o = ps_s[:, t // 4, t % 4 * P:(t % 4 + 1) * P]
                return nc.tensor.matmul(o, src[:, t * P:(t + 1) * P], w0_sb[:, s, :], start=False, stop=stop,
                                        skip_group_check=True)

            def sage_bias():
                for t in range(T):
                    nc.tensor.matmul(ps_s[:, t // 4, t % 4 * P:(t % 4 + 1) * P], ones[0:1, :], b0_row[:, :],
                                     start=(t % 4 == 0), stop=False, skip_group_check=True)

            def sage_h(b):
                pe.wait_ge(turned_sb, b * 10 + 2)
                for t in range(T):
                    sage_part(0, t, hT, stop=False)

            def sage(b):
                pe.wait_ge(gather_free, b * T + T + 2)
                turn_features(b, 1, 1, agg)
                for half in range(2):
                    pe.wait_ge(turned_sb, b * 10 + 3 + half)
                    for t in range(4 * half, 4 * half + 4):
                        ins = sage_part(1, t, aggT, stop=(t % 4 == 3))
                    ins.then_inc(sage_ps, 1)

            def beside(b, layer, i, more2):
                if (layer, i) in CODES:
                    if i == 0:
                        pe.wait_ge(exp_in_ready, b * 6 + 2 * layer)
                    for at in ahead(b, CODES[layer, i], more2):
                        make_codes(*at)
                if (layer, i) in TURNS:
                    for at in ahead(b, TURNS[layer, i], more2):
                        turn_mask(*at)

            def attention(b, layer, more, more2):
                H, D1 = HEADS[layer], width(layer)
                m = b * 3 + (layer - 1)
                WW = C + 3 * H

                def spread_s1(g):
                    k = G0[layer] + g
                    for half in range(2):
                        ins = nc.tensor.matmul(s1_row(k)[:, half, :], wa1[layer][:, g, :],
                                               hT[:, half * 512:(half + 1) * 512], start=True, stop=True)
                    ins.then_inc(s1_ps, 1)

                for half in range(2):
                    turn_features(b, layer + 1, half, h, b * (3 * T) + (B + layer - 1) * T)
                for t in range(T):
                    n = b * 24 + 8 * (layer - 1) + t
                    if t % 4 == 0:
                        pe.wait_ge(turned_sb, b * 10 + 2 * layer + 3 + t // 4)
                    if t >= 2:
                        pe.wait_ge(wh_sb, n - 1)
                    o = ps_w[t % 2][:, 0:WW]
                    if layer > 1 and t < 2:
                        pe.wait_ge(acc_used, b * NA + A0[layer] + t - 1)
                    nc.tensor.matmul(o, hT[:, t * P:(t + 1) * P], wr[layer][:, :], start=True, stop=True)\
                      .then_inc(wh_ps, 1)
                pe.wait_ge(top_ready, m + 1)
                nc.tensor.transpose(ps_small[0:H, 0:P], top_s2[:, 0:H], ident[:, :]).then_inc(top_turned, 1)
                pe.wait_ge(top_diag_ready, m + 1)
                nc.tensor.matmul(ps_small[:, 0:H], ones[0:H, :], top_diag[0:H, 0:H], start=True, stop=True)\
                  .then_inc(top_spread, 1)
                for g in range(min(H, 2)):
                    spread_s1(g)
                if layer == 2:
                    pe.wait_ge(edges_ready, b * (NG * T) + (G0[layer] + 1) * T)
                    spread_s1(2)
                    pe.wait_ge(rough_ready, b * NR + rough_count(G0[2] + 1, T - 1))
                    spread_s1(3)
                if more and layer == 3:
                    sage_bias()
                WJ = 2 * H * D1
                HG = H // GROUPS[layer]
                for i in range(GROUPS[layer] * T):
                    if more:
                        beside(b, layer, i, more2)
                    if more and layer == 3 and i in H0_TURNS:
                        turn_early(b + 1, H0_TURNS.index(i))
                    t, g0 = i % T, i // T * HG
                    n = b * NA + A0[layer] + i
                    if i >= 2:
                        pe.wait_ge(acc_used, n - 1)
                    acc = ps_acc[:, i % 2, 0:2 * HG * D1]
                    acc_v = acc.rearrange("p (h s d) -> p h s d", h=HG, s=2)
                    for j in range(T):
                        if i == 0 and j % TC == 0:
                            pe.wait_ge(nparts_ready, b * (3 * CH) + CH * (layer - 1) + j // TC + 1)
                        if t == 0:
                            pe.wait_ge(edges_ready, b * (NG * T) + (G0[layer] + g0 + HG - 1) * T + j + 1)
                        for g in range(HG):
                            for k in range(3):
                                at = j * WJ + (g0 + g) * 2 * D1
                                nc.tensor.matmul(acc[:, g * 2 * D1:(g + 1) * 2 * D1],
                                                 edges[:, g0 + g, j, t * P:(t + 1) * P], part[:, k, at:at + 2 * D1],
                                                 start=(j == g == k == 0), stop=False, skip_group_check=True)
                        for k in range(3):
                            at = j * (WJ // 2) + g0 * D1
                            ins = nc.tensor.matmul(acc_v[:, :, 1, :], mask[:, j, t * P:(t + 1) * P],
                                                   npart[:, k, at:at + HG * D1].rearrange("p (h d) -> p h d", h=HG),
                                                   start=False, stop=(j == T - 1 and k == 2), skip_group_check=True)
                    ins.then_inc(acc_ready, 1)

            def turn(b, more, more2):
                sage(b)
                for layer in (1, 2, 3):
                    if more:
                        beside(b, layer, -1, more2)
                    attention(b, layer, more, more2)
                if more:
                    turn_early(b + 1, 2)
                    sage_h(b + 1)

            pe.wait_ge(diag_ready, 9)
            for t in range(SLOTS):
                turn_mask(0, t)
                make_codes(0, t)
            pe.wait_ge(weights_in, 16 * (11 + 2 * HM))
            for n, l in enumerate((1, 3)):
                nc.tensor.transpose(ps_x[:, n, 0:C], wr[l][:, 0:C], ident[:, :]).then_inc(wprep_ps, 1)
                pe.wait_ge(wprep_sb, n + 1)
                nc.tensor.matmul(ps_wa[n][:, 0:2], w_turned[n], aggT[:, 2 * l:2 * l + 2],
                                 start=True, stop=True).then_inc(wprep_ps, 1)
            block_diag = aggT[:, 16:16 + 2 * HM]
            nc.tensor.matmul(ps_wa[2][:, 0:2 * HM], hT[:, 0:C], block_diag, start=True, stop=True)
            nc.tensor.matmul(ps_wa[2][0:1, 64:64 + 2 * HM], b2_col[:, 0:1], block_diag, start=True, stop=True)
            pe.wait_ge(wprep_sb, 1)
            nc.tensor.transpose(ps_x[:, 0, 0:C], hT[:, 0:C], ident[:, :]).then_inc(wprep_ps, 1)
            pe.wait_ge(wprep_sb, 3)
            nc.tensor.matmul(ps_x[:, 1, 0:C + 3 * HM], ones[0:1, :], b2_row[:, :], start=True, stop=True)\
              .then_inc(wprep_ps, 1)
            for t in range(SLOTS, T):
                turn_mask(0, t)
                make_codes(0, t)
            pe.wait_ge(weights_ready, NG)
            turn_early(0, 0)
            turn_early(0, 1)
            turn_mask(1, 0)
            make_codes(1, 0)
            turn_early(0, 2)
            sage_bias()
            sage_h(0)
            for t in range(1, EARLY):
                turn_mask(1, t)
                make_codes(1, t)
            turn_mask(1, EARLY)
            with pe.Fori(0, B - 2) as b:
                turn(b, True, True)
            turn(B - 2, True, False)
            turn(B - 1, False, False)


_INS = ['x', 'adj', 'L0_gnn_W', 'L0_gnn_b', 'L1_gnn_W', 'L1_gnn_a', 'L2_gnn_W', 'L2_gnn_b', 'L2_gnn_a', 'L3_gnn_W',
        'L3_gnn_a']
_OUTS = [((8, 1024, 128), 'float32')]


def kernel(**inputs):
    import numpy as _np
    import concourse.bacc as _bacc
    from concourse import mybir as _mybir
    from concourse.bass_utils import run_bass_kernel_spmd as _run

    nc = _bacc.Bacc("TRN2", target_bir_lowering=False, num_devices=1)
    arrays, args = {}, []
    for name in _INS:
        a = _np.ascontiguousarray(inputs[name])
        arrays[f"in_{name}_dram"] = a
        args.append(nc.dram_tensor(f"in_{name}_dram", a.shape, _mybir.dt.from_np(a.dtype), kind="ExternalInput").ap())
    for i, (shape, dtype) in enumerate(_OUTS):
        dt = _mybir.dt.from_np(_np.dtype(dtype))
        args.append(nc.dram_tensor(f"out_{i}_dram", shape, dt, kind="ExternalOutput").ap())
    graph_layers(nc, *args)
    r = _run(nc, [arrays], core_ids=[0])
    got = tuple(r.results[0][f"out_{i}_dram"] for i in range(len(_OUTS)))
    return got[0]
```
